# Optimizing a Trainium2 kernel written in Bass

```python
import numpy as np
import jax
import jax.numpy as jnp

def _softmax(x, axis=-1):
    return jax.nn.softmax(x, axis=axis)

def _gelu(x):
    return jax.nn.gelu(x, approximate=True)

def _silu(x):
    return jax.nn.silu(x)

def _sigmoid(x):
    return jax.nn.sigmoid(x)

def _layernorm(x, axis=-1, eps=1e-05):
    m = jnp.mean(x, axis=axis, keepdims=True)
    v = jnp.var(x, axis=axis, keepdims=True)
    return (x - m) / jnp.sqrt(v + eps)

def _scatter_add(tgt, idx, src, axis=0):
    return tgt.at[idx].add(src)

def _segment_sum(src, seg, n):
    return jax.ops.segment_sum(src, seg, n)
kernel_name = 'mk_cond_resid_d2_seqx_r4_d364fd'

def setup_inputs(seed: int=0):
    np.random.seed(seed)
    _w = jnp.asarray

    def _rec_inputs():
        import jax
        import jax.numpy as jnp
        _rk = jax.random.key(seed)
        x = -0.0002928 + 1 * jax.random.normal(jax.random.fold_in(_rk, 1), (32, 256, 256), jnp.float32)
        _lenS = 256 - jax.random.randint(jax.random.fold_in(_rk, 7), (32,), 0, max(1, 256 // 4) + 1, jnp.int32)
        _lenS2 = 256 - jax.random.randint(jax.random.fold_in(_rk, 8), (32,), 0, max(1, 256 // 4) + 1, jnp.int32)
        cond_1024 = 0.000887014 + 1.03683 * jax.random.normal(jax.random.fold_in(_rk, 11), (32, 256), jnp.float32)
        return (x, cond_1024)
    x, cond_1024 = _rec_inputs()

    def _L0_cond_setup():
        import jax, jax.numpy as jnp
        import numpy as np
        TOP_K = 2
        N_EXPERTS = 8
        N_SHARED = 1
        EPS = 1e-09
        key = jax.random.key(seed)
        ks = jax.random.split(key, 10)
        B, T, d = (2, 512, 256)
        h_s, h_r, E = (512, 128, N_EXPERTS)
        return {'x': jax.random.normal(ks[0], (B, T, d), jnp.float32), 't_emb': jax.random.normal(ks[1], (B, d), jnp.float32), 'router_w': jax.random.normal(ks[2], (E, d), jnp.float32) * 0.01, 'router_t_w': jax.random.normal(ks[3], (E, d), jnp.float32) * 0.01, 'router_bias': jnp.zeros((E,), jnp.float32), 'sw1': jax.random.normal(ks[4], (h_s, d), jnp.float32) * 0.02, 'sw3': jax.random.normal(ks[5], (h_s, d), jnp.float32) * 0.02, 'sw2': jax.random.normal(ks[6], (d, h_s), jnp.float32) * 0.02, 'rw1': jax.random.normal(ks[7], (E, h_r, d), jnp.float32) * 0.02, 'rw2': jax.random.normal(ks[8], (E, d, h_r), jnp.float32) * 0.02}
    _L0_cond_all = _L0_cond_setup()
    _L0_cond_in = {k: v for k, v in _L0_cond_all.items() if k in ('router_w', 'router_t_w', 'router_bias', 'sw1', 'sw3', 'sw2', 'rw1', 'rw2')}
    del _L0_cond_all

    def _L1_cond_setup():
        import jax, jax.numpy as jnp
        import numpy as np
        N, T, D, H = (64, 128, 256, 256)
        key = jax.random.key(seed)
        k1, k2, k3, k4 = jax.random.split(key, 4)
        x = jax.random.normal(k1, (N, T, D), dtype=jnp.float32)
        h0 = jax.random.normal(k2, (N, H), dtype=jnp.float32)
        Wx = jax.random.normal(k3, (D, H), dtype=jnp.float32) / np.sqrt(D)
        Wh = jax.random.normal(k4, (H, H), dtype=jnp.float32) / np.sqrt(H)
        b = jnp.zeros((H,), dtype=jnp.float32)
        return {'x': x, 'h0': h0, 'Wx': Wx, 'Wh': Wh, 'b': b}
    _L1_cond_all = _L1_cond_setup()
    _L1_cond_in = {k: v for k, v in _L1_cond_all.items() if k in ('Wx', 'Wh', 'b')}
    del _L1_cond_all
    return {'x': x, 'cond_1024': cond_1024, 'L0_cond_router_w': _L0_cond_in['router_w'], 'L0_cond_router_t_w': _L0_cond_in['router_t_w'], 'L0_cond_router_bias': _L0_cond_in['router_bias'], 'L0_cond_sw1': _L0_cond_in['sw1'], 'L0_cond_sw3': _L0_cond_in['sw3'], 'L0_cond_sw2': _L0_cond_in['sw2'], 'L0_cond_rw1': _L0_cond_in['rw1'], 'L0_cond_rw2': _L0_cond_in['rw2'], 'L1_cond_Wx': _L1_cond_in['Wx'], 'L1_cond_Wh': _L1_cond_in['Wh'], 'L1_cond_b': _L1_cond_in['b']}

def reference(x, cond_1024, L0_cond_router_w, L0_cond_router_t_w, L0_cond_router_bias, L0_cond_sw1, L0_cond_sw3, L0_cond_sw2, L0_cond_rw1, L0_cond_rw2, L1_cond_Wx, L1_cond_Wh, L1_cond_b):
    import jax
    import jax.numpy as jnp

    def _L0_cond_ref(x, t_emb, router_w, router_t_w, router_bias, sw1, sw3, sw2, rw1, rw2):
        import jax, jax.numpy as jnp
        import numpy as np
        TOP_K = 2
        N_EXPERTS = 8
        N_SHARED = 1
        EPS = 1e-09
        B, T, C = x.shape
        N = B * T
        x_flat = x.reshape(N, C)
        shared_out = jnp.einsum('nh,dh->nd', jax.nn.silu(x_flat @ sw1.T) * (x_flat @ sw3.T), sw2)
        t_bias = t_emb @ router_t_w.T
        t_bias_flat = jnp.broadcast_to(t_bias[:, None, :], (B, T, N_EXPERTS)).reshape(N, N_EXPERTS)
        s = jax.nn.sigmoid((x_flat @ router_w.T + t_bias_flat).astype(jnp.float32))
        sel_scores = s + router_bias
        _, topk_idx = jax.lax.top_k(sel_scores, TOP_K)
        s_sel = jnp.take_along_axis(s, topk_idx, axis=1)
        denom = jnp.sum(s_sel, axis=1, keepdims=True)
        gates = jnp.where(denom > EPS, s_sel / (denom + EPS), 1.0 / TOP_K).astype(x.dtype)
        combine = jnp.sum(gates[:, :, None] * jax.nn.one_hot(topk_idx, N_EXPERTS, dtype=x.dtype), axis=1)
        H = jax.nn.gelu(jnp.einsum('nd,ehd->enh', x_flat, rw1), approximate=False)
        O = jnp.einsum('enh,edh->end', H, rw2)
        routed_out = jnp.einsum('end,ne->nd', O, combine)
        out = (shared_out + routed_out) / (N_SHARED + TOP_K)
        return out.reshape(B, T, C)

    def _L1_cond_ref(x, h0, Wx, Wh, b):
        import jax, jax.numpy as jnp
        import numpy as np
        N, T, D, H = (64, 128, 256, 256)
        xW = jnp.einsum('ntd,dh->nth', x, Wx) + b
        xW_t = jnp.swapaxes(xW, 0, 1)

        def step(prev_h, xw):
            next_h = jnp.tanh(prev_h @ Wh + xw)
            return (next_h, next_h)
        _, h_t = jax.lax.scan(step, h0, xW_t)
        return jnp.swapaxes(h_t, 0, 1)
    x = x + _L0_cond_ref(x, cond_1024, L0_cond_router_w, L0_cond_router_t_w, L0_cond_router_bias, L0_cond_sw1, L0_cond_sw3, L0_cond_sw2, L0_cond_rw1, L0_cond_rw2)
    x = x + _L1_cond_ref(x, cond_1024, L1_cond_Wx, L1_cond_Wh, L1_cond_b)
    return x

_drawn_inputs = setup_inputs


def setup_inputs(seed=0):
    import zlib

    import numpy as np

    out = dict(_drawn_inputs(seed))
    spreads = {'L0_cond_router_bias': (0.0, 0.757), 'L1_cond_b': (0.0, 0.687)}
    factors = {'L0_cond_router_w': 8.0,
     'L0_cond_router_t_w': 8.0,
     'L0_cond_sw1': 6.719,
     'L0_cond_sw3': 6.653,
     'L0_cond_sw2': 6.626,
     'L0_cond_rw1': 5.898,
     'L0_cond_rw2': 5.776}
    for name, (base, spread) in spreads.items():
        noise = np.random.default_rng([zlib.crc32(name.encode()), seed]).standard_normal(out[name].shape)
        drawn = base * np.exp(spread * noise) if base else spread * noise
        out[name] = jnp.asarray(drawn.astype(out[name].dtype))
    for name, factor in factors.items():
        out[name] = (out[name] * factor).astype(out[name].dtype)
    return out
```

```python
from contextlib import ExitStack

import concourse.bass as bass
from concourse import mybir

F32 = mybir.dt.float32
F32R = mybir.dt.float32r
BF16 = mybir.dt.bfloat16
F16 = mybir.dt.float16
ALU = mybir.AluOpType
ACT = mybir.ActivationFunctionType
AX = mybir.AxisListType

P = 128
BATCH, TIME, DIM = 32, 256, 256
EXPERTS = 8
HIDDEN_SHARED = 512
STEPS = 16
TOK = STEPS * BATCH
CHUNKS = TIME // STEPS
KT = DIM // P
SHARED = HIDDEN_SHARED // P
BLOCKS = SHARED + EXPERTS
TILES = 2 * SHARED + EXPERTS
LAG = 4
EPS = 1e-9
SCALE = 4096.0
PRODUCTS = [[0, 1, 2], [0, 1]]
BIAS_ROWS = 96
RING = [0, 1, 2] * 5 + [1]
W1, W3, W2, R1, R2, WX = 0, 1024, 2048, 3072, 5120, 7168
W_COLS = 7680
GROUP = 1024
GROUPS = [(a, min(a + GROUP, W_COLS)) for a in range(0, W_COLS, GROUP)]
WH, COND, RW, RT, RB, RANK = 0, 512, 576, 592, 608, 616
S_COLS = 624
DOWN = {0: [(10, (0, 1), 1)], 1: [(11, (0, 1), 1)],
        4: [(0, (0,), 0)], 5: [(0, (1,), 0)], 6: [(1, (0,), 0)], 7: [(1, (1,), 0)],
        8: [(2, (0, 1), 0)], 9: [(3, (0, 1), 0)],
        **{10 + e: [(4 + e, (0, 1), 0)] for e in range(6)}}
ROUTER_OPS = 27
LOGIT_OPS = 3


def moe_rnn(nc, x_in, w_in, s_in, b_in, scratch, out):
    with ExitStack() as ctx:
        def sb(name, shape, dt=F32):
            return ctx.enter_context(nc.sbuf_tensor(name, shape, dt))

        def pb(name, shape):
            return ctx.enter_context(nc.psum_tensor(name, shape, F32))

        def sem(name):
            return ctx.enter_context(nc.semaphore(name))

        w_raw = sb("w_raw", [P, W_COLS - 4 * GROUP])
        w_hi = sb("w_hi", [P, W_COLS], F32R)
        w_lo = sb("w_lo", [P, W_COLS], F32R)
        small = sb("small", [P, S_COLS])
        x = [sb(f"x{p}", [P, KT, TOK]) for p in range(2)]
        x_hi = [sb(f"x_hi{p}", [P, KT, TOK], F32R) for p in range(2)]
        x_lo = [sb(f"x_lo{p}", [P, KT, TOK], F32R) for p in range(2)]
        x1 = [sb(f"x1_{p}", [P, KT, TOK]) for p in range(2)]
        x1_hi = sb("x1_hi", [P, KT, TOK], F32R)
        x1_lo = sb("x1_lo", [P, KT, TOK], F32R)
        h = [sb(f"h{p}", [P, KT, TOK]) for p in range(2)]
        h_part = [[sb(f"h_part{n}_{s}", [P, KT, BATCH], F16) for s in range(2)] for n in range(2)]
        wh_part = [sb(f"wh_part{n}", [P, KT * DIM], BF16) for n in range(3)]
        wh_rest = sb("wh_rest", [P, KT * DIM])
        b_raw = sb("b_raw", [BIAS_ROWS, DIM])
        b_part = [sb(f"b_part{n}", [BIAS_ROWS, DIM], BF16) for n in range(3)]
        b_rows = sb("b_rows", [BIAS_ROWS, DIM], BF16)
        ones = sb("ones", [BIAS_ROWS, TOK], BF16)
        gate_bc = [sb(f"gate_bc{p}", [P, EXPERTS, TOK]) for p in range(2)]
        g = [sb(f"g{i}", [P, TOK]) for i in range(2)]
        u = sb("u", [P, TOK])
        hs = [sb(f"hs{i}", [P, TOK]) for i in range(2)]
        hs_hi = [sb(f"hs_hi{i}", [P, TOK], F32R) for i in range(3)]
        hs_lo = [sb(f"hs_lo{i}", [P, TOK], F32R) for i in range(3)]
        rw_pad = sb("rw_pad", [P, KT, P], F32R)
        t_bias = sb("t_bias", [BATCH, EXPERTS])
        route_t = sb("route_t", [BATCH, STEPS, 32])
        logit = sb("logit", [BATCH, STEPS, EXPERTS])
        score = sb("score", [BATCH, STEPS, EXPERTS])
        sel = sb("sel", [BATCH, STEPS, EXPERTS])
        hit = sb("hit", [BATCH, STEPS, EXPERTS])
        first = sb("first", [BATCH, STEPS, EXPERTS])
        second = sb("second", [BATCH, STEPS, EXPERTS])
        top = sb("top", [BATCH, STEPS])
        den = sb("den", [BATCH, STEPS])
        inv = sb("inv", [BATCH, STEPS])
        big = sb("big", [BATCH, STEPS])
        comb = sb("comb", [BATCH, STEPS, 32])
        comb_t = [sb(f"comb_t{p}", [32, TOK]) for p in range(2)]
        gelu_probe = sb("gelu_probe", [BATCH, 1])

        up = [pb(f"up{i}", [P, TOK]) for i in range(3)]
        acc = [pb(f"acc{m}", [P, TOK]) for m in range(KT)]
        rec = pb("rec", [P, KT, TOK])
        route = pb("route", [P, 512])

        small_loaded = sem("small_loaded")
        w_loaded = [sem(f"w_loaded{i}") for i in range(len(GROUPS))]
        x_loaded = [sem(f"x_loaded{p}") for p in range(2)]
        comb_stored = sem("comb_stored")
        gate_loaded = [sem(f"gate_loaded{p}") for p in range(2)]
        out_stored = [sem(f"out_stored{p}") for p in range(2)]
        w_hi_done = sem("w_hi_done")
        w_lo_done = sem("w_lo_done")
        w_rest_done = sem("w_rest_done")
        rw_cleared = sem("rw_cleared")
        rw_hi_done = sem("rw_hi_done")
        rw_lo_done = sem("rw_lo_done")
        comb_cleared = sem("comb_cleared")
        x_hi_done = sem("x_hi_done")
        x_lo_done = sem("x_lo_done")
        t_bias_done = sem("t_bias_done")
        t_bias_copied = sem("t_bias_copied")
        route_done = sem("route_done")
        score_done = sem("score_done")
        router_step = sem("router_step")
        up_done = sem("up_done")
        down_done = sem("down_done")
        act_done = sem("act_done")
        u_done = sem("u_done")
        hs_done = sem("hs_done")
        hi_done = sem("hi_done")
        lo_done = sem("lo_done")
        x1_done = sem("x1_done")
        x1_hi_done = sem("x1_hi_done")
        x1_lo_done = sem("x1_lo_done")
        wx_done = sem("wx_done")
        rec_done = sem("rec_done")
        h_done = sem("h_done")
        part_done = [sem(f"part{n}_done") for n in range(2)]
        b_loaded = sem("b_loaded")
        wh_step = sem("wh_step")
        b_step = sem("b_step")
        out_done = sem("out_done")

        block = ctx.enter_context(nc.Block())

        def schedule(eng, prologue, body):
            prologue()
            body(0, 0, new=True, one=False, two=False, nxt=True)
            body(1, 1, new=True, one=True, two=False, nxt=True)
            body(2, 0, new=True, one=True, two=True, nxt=True)
            with eng.Fori(1, CHUNKS // 2 - 1) as pair:
                body(pair * 2 + 1, 1, new=True, one=True, two=True, nxt=True)
                body(pair * 2 + 2, 0, new=True, one=True, two=True, nxt=True)
            body(CHUNKS - 1, 1, new=True, one=True, two=True, nxt=False)
            body(CHUNKS, 0, new=False, one=True, two=True, nxt=False)
            body(CHUNKS + 1, 1, new=False, one=False, two=True, nxt=False)

        def steps_of(c, i, one, two):
            if known(c, CHUNKS - 1):
                if i < LAG:
                    return [(2, STEPS - LAG + i)]
                if i < 8:
                    return [(1, i - LAG)]
                r = i - LAG + (i - 7) // 2
                return [(1, r)] if i % 2 else [(1, r), (1, r + 1)]
            if i < LAG:
                return [(2, STEPS - LAG + i)] if two and not known(c, CHUNKS) else []
            return [(1, i - LAG)] if one else []

        def raw(n):
            a, b = GROUPS[n]
            if R1 <= a < WX:
                return gate_bc[1][:, :, :].rearrange("p e n -> p (e n)")[:, a - R1:b - R1]
            return w_raw[:, a:b] if a < R1 else w_raw[:, a - 4 * GROUP:b - 4 * GROUP]

        def known(c, n):
            return isinstance(c, int) and c == n

        def below(c, n):
            return isinstance(c, int) and c < n

        def nth(c, par):
            return c * 8 + (16 - 8 * par)

        @block.sync
        def _(sp):
            def load_x(c, par):
                sp.dma_start(x[par][:, :, :], x_in[bass.ts(c, P), :].rearrange("p (k n) -> p k n", k=KT)
                             ).then_inc(x_loaded[par], 16)

            def load_w(n):
                a, b = GROUPS[n]
                sp.dma_start(raw(n), w_in[:, a:b]).then_inc(w_loaded[n], 16)

            def gates(c, par):
                sp.wait_ge(router_step, c * ROUTER_OPS + ROUTER_OPS)
                if not below(c, 2):
                    sp.wait_ge(gate_loaded[par], nth(c - 2, par))
                rows = scratch[par * EXPERTS:(par + 1) * EXPERTS, :]
                sp.dma_start(rows, comb_t[par][0:EXPERTS, :]).then_inc(comb_stored, 16)
                sp.wait_ge(comb_stored, c * 16 + 16)
                if not below(c, 2):
                    sp.wait_ge(hs_done, c * BLOCKS - BLOCKS)
                if known(c, 1):
                    sp.wait_ge(w_rest_done, 5)
                flat = rows.rearrange("(o e) n -> o (e n)", o=1)
                sp.dma_start(gate_bc[par][:, :, :].rearrange("p e n -> p (e n)"),
                             flat.broadcast_to([P, EXPERTS * TOK])).then_inc(gate_loaded[par], 16)

            def prologue():
                load_x(0, 0)
                load_w(0)
                load_w(1)
                load_x(1, 1)
                for n in range(2, len(GROUPS)):
                    load_w(n)

            def body(c, par, new, one, two, nxt):
                if known(c, 0):
                    gates(0, 0)
                if nxt and not known(c, 0):
                    sp.wait_ge(x1_done, c * KT)
                    load_x(c + 1, 1 - par)
                if two:
                    sp.wait_ge(out_done, c - 1)
                    sp.dma_start(out[bass.ts(c - 2, P), :].rearrange("p (k n) -> p k n", k=KT),
                                 x1[par][:, :, :]).then_inc(out_stored[par], 16)
                if nxt:
                    gates(c + 1, 1 - par)

            schedule(sp, prologue, body)
            for par in range(2):
                sp.wait_ge(out_stored[par], 16 * (CHUNKS // 2))

        @block.tensor
        def _(pe):
            def three(dst, col, hi, lo, start, stop, inc=None):
                wh, wl = w_hi[:, col:col + P], w_lo[:, col:col + P]
                pe.matmul(dst, wh, hi, start=start, stop=False, skip_group_check=True)
                pe.matmul(dst, wh, lo, start=False, stop=False, skip_group_check=True)
                mm = pe.matmul(dst, wl, hi, start=False, stop=stop, skip_group_check=True)
                if inc is not None:
                    mm.then_inc(inc, 1)

            def router(c, par):
                if known(c, 0):
                    pe.wait_ge(rw_lo_done, 1)
                    pe.wait_ge(t_bias_copied, 1)
                else:
                    pe.wait_ge(router_step, c * ROUTER_OPS + (1 - ROUTER_OPS))
                    pe.wait_ge(x_lo_done, c + 1)
                for k in range(KT):
                    for part in (x_hi, x_lo):
                        mm = pe.matmul(route[:, :], rw_pad[:, k, :], part[par][:, k, :],
                                       start=(k == 0 and part is x_hi),
                                       stop=(k == KT - 1 and part is x_lo))
                mm.then_inc(route_done, 1)

            def recur(q, r):
                cols = slice(r * BATCH, (r + 1) * BATCH)
                if known(q, 0) and r == 0:
                    pe.wait_ge(small_loaded, 16)
                    for m in range(KT):
                        for k in range(KT):
                            mm = pe.matmul(rec[:, m, cols],
                                           small[:, WH + k * DIM + m * P:WH + k * DIM + (m + 1) * P],
                                           small[:, COND + k * BATCH:COND + (k + 1) * BATCH],
                                           start=False, stop=(k == KT - 1), skip_group_check=True)
                    mm.then_inc(rec_done, 1)
                    return
                if known(q, 0) and r == 1:
                    pe.wait_ge(wh_step, 5)
                for n in range(2):
                    pe.wait_ge(part_done[n], q * STEPS + r)
                    for m in range(KT):
                        for k in range(KT):
                            for w in PRODUCTS[n]:
                                mm = pe.matmul(rec[:, m, cols],
                                               wh_part[w][:, k * DIM + m * P:k * DIM + (m + 1) * P],
                                               h_part[n][(r - 1) % 2][:, k, :], start=False,
                                               stop=(n == 1 and k == KT - 1 and w == PRODUCTS[1][-1]),
                                               skip_group_check=True)
                mm.then_inc(rec_done, 1)

            def input_part(q):
                if known(q, 0):
                    pe.wait_ge(b_step, 10)
                else:
                    pe.wait_ge(h_done, q * STEPS)
                for m in range(KT):
                    pe.matmul(rec[:, m, :], b_rows[:, m * P:(m + 1) * P], ones[:, :],
                              start=True, stop=False, skip_group_check=True)
                for k in range(KT):
                    pe.wait_ge(x1_lo_done, q * KT + (k + 1))
                    for m in range(KT):
                        last = k == KT - 1 and m == KT - 1
                        three(rec[:, m, :], WX + k * DIM + m * P, x1_hi[:, k, :], x1_lo[:, k, :],
                              False, False, wx_done if last else None)

            def up_waits(c, i):
                back, prev = 0, i - 1
                while RING[prev % TILES] != RING[i]:
                    prev -= 1
                if prev < 0:
                    back, prev = 1, prev + TILES
                if not (known(c, 0) and back):
                    if prev >= 2 * SHARED:
                        pe.wait_ge(act_done, c * BLOCKS + (prev - SHARED + 1 - back * BLOCKS))
                    elif prev % 2:
                        pe.wait_ge(hs_done, c * BLOCKS + (prev // 2 + 1 - back * BLOCKS))
                    else:
                        pe.wait_ge(u_done, c * SHARED + (prev // 2 + 1 - back * SHARED))
                if i == 0:
                    pe.wait_ge(x_lo_done, c + 1)
                if known(c, 0):
                    if i < 2:
                        pe.wait_ge(w_lo_done, i + 1)
                    if i in (8, 12):
                        pe.wait_ge(w_rest_done, i // 4)

            def up_tile(c, i, par, ks):
                if ks[0] == 0:
                    up_waits(c, i)
                for k in ks:
                    if i < 2 * SHARED:
                        col = (W3 if i % 2 else W1) + k * HIDDEN_SHARED + (i // 2) * P
                    else:
                        col = R1 + (i - 2 * SHARED) * DIM + k * P
                    three(up[RING[i]][:, :], col, x_hi[par][:, k, :], x_lo[par][:, k, :],
                          k == 0, k == KT - 1, up_done if k == KT - 1 else None)

            def down(c, b, ms):
                if ms[0] == 0:
                    pe.wait_ge(lo_done, c * BLOCKS + (b + 1))
                    if b == 0 and not known(c, 0):
                        pe.wait_ge(x1_done, c * KT)
                    if known(c, 0) and b in (0, 4, 8):
                        pe.wait_ge(w_rest_done, {0: 1, 4: 4, 8: 5}[b])
                for m in ms:
                    col = (W2 + b * DIM if b < SHARED else R2 + (b - SHARED) * DIM) + m * P
                    three(acc[m][:, :], col, hs_hi[b % 3][:, :], hs_lo[b % 3][:, :],
                          b == 0, b == BLOCKS - 1, down_done if m == KT - 1 else None)

            def prologue():
                pe.wait_ge(small_loaded, 16)
                for k in range(KT):
                    mm = pe.matmul(route[0:BATCH, 0:EXPERTS],
                                   small[:, COND + k * BATCH:COND + (k + 1) * BATCH],
                                   small[:, RT + k * EXPERTS:RT + (k + 1) * EXPERTS],
                                   start=(k == 0), stop=(k == KT - 1))
                mm.then_inc(t_bias_done, 1)

            def body(c, par, new, one, two, nxt):
                for i in range(STEPS):
                    steps = steps_of(c, i, one, two)
                    for back, r in steps[:1]:
                        recur(c - back, r)
                    if new and i == 3:
                        up_tile(c, 3, par, (1,))
                    elif new:
                        up_tile(c, i, par, (0, 1))
                    if new and i == 2:
                        up_tile(c, 3, par, (0,))
                    for back, r in steps[1:]:
                        recur(c - back, r)
                    if i == 1 and known(c, 0):
                        router(0, 0)
                    for b, ms, back in DOWN.get(i, []):
                        if back and one:
                            down(c - 1, b, ms)
                        if not back and new:
                            down(c, b, ms)
                    if i == LAG - 1 and one:
                        if known(c, 1):
                            pe.wait_ge(w_rest_done, 6)
                        input_part(c - 1)
                    if i == LAG + 1 and nxt:
                        router(c + 1, 1 - par)

            schedule(pe, prologue, body)

        @block.scalar
        def _(act):
            def split_w(n):
                a, b = GROUPS[n]
                act.wait_ge(w_loaded[n], 16)
                act.copy(w_hi[:, a:b], raw(n)).then_inc(w_hi_done, 1)

            def split_x(c, par):
                act.wait_ge(x_loaded[par], nth(c, par))
                if not below(c, 2):
                    act.wait_ge(up_done, c * TILES - TILES)
                act.copy(x_hi[par][:, :, :], x[par][:, :, :]).then_inc(x_hi_done, 1)

            def squash(c, b):
                tile = 2 * b if b < SHARED else b + SHARED
                act.wait_ge(up_done, c * TILES + (tile + 1))
                if not (known(c, 0) and b < 2):
                    act.wait_ge(hs_done, c * BLOCKS + (b - 1))
                if b < SHARED:
                    ins = act.activation(g[b % 2][:, :], up[RING[tile]][:, :], ACT.Tanh, scale=0.5)
                else:
                    ins = act.activation(g[b % 2][:, :], up[RING[tile]][:, :], ACT.Gelu)
                ins.then_inc(act_done, 1)

            def high(c, b):
                act.wait_ge(hs_done, c * BLOCKS + (b + 1))
                if not (known(c, 0) and b < 3):
                    act.wait_ge(down_done, c * BLOCKS + (b - 2))
                act.copy(hs_hi[b % 3][:, :], hs[b % 2][:, :]).then_inc(hi_done, 1)

            def recur(q, r, par):
                if r == 0 and not below(q, 2):
                    act.wait_ge(out_done, q - 1)
                act.wait_ge(rec_done, q * STEPS + (r + 1))
                cols = slice(r * BATCH, (r + 1) * BATCH)
                act.activation(h[par][:, :, cols], rec[:, :, cols], ACT.Tanh).then_inc(h_done, 1)

            def sigmoid(c):
                act.wait_ge(router_step, c * ROUTER_OPS + LOGIT_OPS)
                act.activation(score[:, :, :], logit[:, :, :], ACT.Sigmoid).then_inc(score_done, 1)

            def load_gelu(c):
                act.wait_ge(score_done, c + 1)
                act.activation(gelu_probe[:, :], score[:, 0, 0:1], ACT.Gelu)

            def prologue():
                act.dma_start(small[:, :], s_in[:, :]).then_inc(small_loaded, 16)
                act.dma_start(b_raw[:, :], b_in.broadcast_to([BIAS_ROWS, DIM])).then_inc(b_loaded, 16)
                split_x(0, 0)
                split_w(0)
                split_w(1)
                act.wait_ge(rw_cleared, 1)
                act.wait_ge(small_loaded, 16)
                act.copy(rw_pad[:, :, 0:EXPERTS],
                         small[:, RW:RW + KT * EXPERTS].rearrange("p (k e) -> p k e", k=KT)
                         ).then_inc(rw_hi_done, 1)

            def body(c, par, new, one, two, nxt):
                for i in range(STEPS):
                    if i == 0 and one:
                        squash(c - 1, BLOCKS - 1)
                    if new and i in (1, 3, 5, 7):
                        squash(c, i // 2)
                    if new and i > 8:
                        squash(c, SHARED + i - 9)
                    steps = steps_of(c, i, one, two)
                    for back, r in steps[:1]:
                        recur(c - back, r, par if back == 2 else 1 - par)
                    if i == 0 and one:
                        high(c - 1, BLOCKS - 1)
                    if i == 2 and one:
                        for k in range(KT):
                            act.wait_ge(x1_done, c * KT - KT + (k + 1))
                            if not known(c, 1):
                                act.wait_ge(wx_done, c - 1)
                            act.copy(x1_hi[:, k, :], x1[1 - par][:, k, :]).then_inc(x1_hi_done, 1)
                    if new and i in (3, 4, 6, 8):
                        high(c, {3: 0, 4: 1, 6: 2, 8: 3}[i])
                    if new and i > 8:
                        high(c, SHARED + i - 9)
                    for back, r in steps[1:]:
                        recur(c - back, r, par if back == 2 else 1 - par)
                    if i == 4 and nxt:
                        split_x(c + 1, 1 - par)
                    if known(c, 0):
                        if i in (0, 2, 3, 5, 6, 8):
                            split_w({0: 2, 2: 3, 3: 4, 5: 5, 6: 6, 8: 7}[i])
                        if i == 2:
                            sigmoid(0)
                    if i == 6 and nxt:
                        sigmoid(c + 1)
                    if i == 7 and nxt:
                        load_gelu(c + 1)

            schedule(act, prologue, body)

        @block.gpsimd
        def _(pool):
            pool.memset(rw_pad[:, :, :].bitcast(F32), 0.0).then_inc(rw_cleared, 1)
            pool.memset(comb[:, :, :], 0.0).then_inc(comb_cleared, 1)
            for n in range(2, len(GROUPS)):
                a, b = GROUPS[n]
                pool.wait_ge(w_hi_done, n + 1)
                pool.tensor_tensor(w_lo[:, a:b], raw(n), w_hi[:, a:b].bitcast(F32), ALU.subtract
                                   ).then_inc(w_rest_done, 1)

        @block.vector
        def _(dve):
            def low_w(n):
                a, b = GROUPS[n]
                dve.wait_ge(w_hi_done, n + 1)
                dve.tensor_tensor(w_lo[:, a:b], raw(n), w_hi[:, a:b].bitcast(F32), ALU.subtract
                                  ).then_inc(w_lo_done, 1)

            def low_x(c, par):
                dve.wait_ge(x_hi_done, c + 1)
                dve.tensor_tensor(x_lo[par][:, :, :], x[par][:, :, :], x_hi[par][:, :, :].bitcast(F32),
                                  ALU.subtract).then_inc(x_lo_done, 1)

            def half_silu(c, j):
                dve.wait_ge(act_done, c * BLOCKS + (j + 1))
                if j:
                    dve.wait_ge(hs_done, c * BLOCKS + j)
                dve.scalar_tensor_tensor(out=u[:, :], in0=g[j % 2][:, :], scalar=1.0,
                                         in1=up[RING[2 * j]][:, :], op0=ALU.add, op1=ALU.mult
                                         ).then_inc(u_done, 1)

            def shared_product(c, j):
                dve.wait_ge(u_done, c * SHARED + (j + 1))
                dve.wait_ge(up_done, c * TILES + (2 * j + 2))
                dve.scalar_tensor_tensor(out=hs[j % 2][:, :], in0=u[:, :], scalar=0.5,
                                         in1=up[RING[2 * j + 1]][:, :], op0=ALU.mult, op1=ALU.mult
                                         ).then_inc(hs_done, 1)

            def routed_product(c, e, par):
                b = SHARED + e
                if e == 0:
                    dve.wait_ge(gate_loaded[par], nth(c, par))
                dve.wait_ge(act_done, c * BLOCKS + (b + 1))
                dve.tensor_tensor(hs[b % 2][:, :], g[b % 2][:, :], gate_bc[par][:, e, :], ALU.mult
                                  ).then_inc(hs_done, 1)

            def low(c, b):
                dve.wait_ge(hi_done, c * BLOCKS + (b + 1))
                dve.tensor_tensor(hs_lo[b % 3][:, :], hs[b % 2][:, :], hs_hi[b % 3][:, :].bitcast(F32),
                                  ALU.subtract).then_inc(lo_done, 1)

            def each(a):
                return a.rearrange("p (t o) -> p t o", o=1).broadcast_to([BATCH, STEPS, EXPERTS])

            def per_expert(a):
                return a.rearrange("p (o e) -> p o e", o=1).broadcast_to([BATCH, STEPS, EXPERTS])

            def logits(c):
                base = c * ROUTER_OPS
                dve.wait_ge(route_done, c + 1)
                if known(c, 0):
                    dve.wait_ge(t_bias_copied, 1)
                dve.transpose(route_t[:, :, :].rearrange("p s r -> p (s r)"), route[0:32, :]
                              ).then_inc(router_step, 1)
                dve.wait_ge(router_step, base + 1)
                dve.tensor_tensor(logit[:, :, :], route_t[:, :, 0:EXPERTS],
                                  route_t[:, :, EXPERTS:2 * EXPERTS], ALU.add).then_inc(router_step, 1)
                dve.wait_ge(router_step, base + 2)
                dve.tensor_tensor(logit[:, :, :], logit[:, :, :], per_expert(t_bias[:, :]), ALU.add
                                  ).then_inc(router_step, 1)

            def selection(c):
                dve.wait_ge(score_done, c + 1)
                dve.tensor_tensor(sel[:, :, :], score[:, :, :],
                                  per_expert(small[0:BATCH, RB:RB + EXPERTS]), ALU.add
                                  ).then_inc(router_step, 1)

            def reach(c, n):
                base = c * ROUTER_OPS + n
                dve.wait_ge(router_step, base)
                dve.tensor_reduce(top[:, :], sel[:, :, :], AX.X, ALU.max).then_inc(router_step, 1)
                dve.wait_ge(router_step, base + 1)
                dve.tensor_tensor(hit[:, :, :], sel[:, :, :], each(top[:, :]), ALU.is_equal
                                  ).then_inc(router_step, 1)
                dve.wait_ge(router_step, base + 2)
                dve.tensor_tensor(hit[:, :, :], hit[:, :, :],
                                  per_expert(small[0:BATCH, RANK:RANK + EXPERTS]), ALU.mult
                                  ).then_inc(router_step, 1)

            def lowest(c, n, one):
                base = c * ROUTER_OPS + n
                dve.wait_ge(router_step, base)
                dve.tensor_reduce(top[:, :], hit[:, :, :], AX.X, ALU.max).then_inc(router_step, 1)
                dve.wait_ge(router_step, base + 1)
                dve.tensor_tensor(one[:, :, :], hit[:, :, :], each(top[:, :]), ALU.is_equal
                                  ).then_inc(router_step, 1)

            def strike_first(c):
                dve.wait_ge(router_step, c * ROUTER_OPS + 9)
                dve.scalar_tensor_tensor(out=sel[:, :, :], in0=first[:, :, :], scalar=-3.0e38,
                                         in1=sel[:, :, :], op0=ALU.mult, op1=ALU.add
                                         ).then_inc(router_step, 1)

            def picked_sum(c):
                base = c * ROUTER_OPS
                dve.wait_ge(router_step, base + 15)
                dve.tensor_tensor(second[:, :, :], first[:, :, :], second[:, :, :], ALU.add
                                  ).then_inc(router_step, 1)
                dve.wait_ge(router_step, base + 16)
                if known(c, 0):
                    dve.wait_ge(comb_cleared, 1)
                dve.tensor_tensor(comb[:, :, 0:EXPERTS], second[:, :, :], score[:, :, :], ALU.mult
                                  ).then_inc(router_step, 1)
                dve.wait_ge(router_step, base + 17)
                dve.tensor_reduce(den[:, :], comb[:, :, 0:EXPERTS], AX.X, ALU.add
                                  ).then_inc(router_step, 1)
                dve.wait_ge(router_step, base + 18)
                dve.tensor_scalar(inv[:, :], den[:, :], EPS, None, ALU.add).then_inc(router_step, 1)
                dve.tensor_scalar(big[:, :], den[:, :], EPS, None, ALU.is_gt).then_inc(router_step, 1)

            def factors(c):
                base = c * ROUTER_OPS
                dve.wait_ge(router_step, base + 19)
                dve.reciprocal(inv[:, :], inv[:, :]).then_inc(router_step, 1)
                dve.wait_ge(router_step, base + 21)
                dve.tensor_tensor(inv[:, :], inv[:, :], big[:, :], ALU.mult).then_inc(router_step, 1)
                dve.tensor_scalar(big[:, :], big[:, :], -0.5, 0.5, ALU.mult, ALU.add
                                  ).then_inc(router_step, 1)

            def combine(c, par):
                base = c * ROUTER_OPS
                dve.wait_ge(router_step, base + 23)
                dve.tensor_tensor(comb[:, :, 0:EXPERTS], comb[:, :, 0:EXPERTS], each(inv[:, :]), ALU.mult
                                  ).then_inc(router_step, 1)
                dve.tensor_tensor(second[:, :, :], second[:, :, :], each(big[:, :]), ALU.mult
                                  ).then_inc(router_step, 1)
                dve.wait_ge(router_step, base + 25)
                dve.tensor_tensor(comb[:, :, 0:EXPERTS], comb[:, :, 0:EXPERTS], second[:, :, :], ALU.add
                                  ).then_inc(router_step, 1)
                dve.wait_ge(router_step, base + 26)
                if not below(c, 2):
                    dve.wait_ge(comb_stored, c * 16 - 16)
                dve.transpose(comb_t[par][:, :], comb[:, :, :].rearrange("p t e -> p (t e)")
                              ).then_inc(router_step, 1)

            def routing(c, par, piece):
                if piece == 0:
                    selection(c)
                    reach(c, 4)
                if piece == 1:
                    lowest(c, 7, first)
                    strike_first(c)
                if piece == 2:
                    reach(c, 10)
                if piece == 3:
                    lowest(c, 13, second)
                if piece == 4:
                    picked_sum(c)
                if piece == 5:
                    factors(c)
                if piece == 6:
                    combine(c, par)

            def residual(c, par, m):
                if m == 0:
                    dve.wait_ge(down_done, c * BLOCKS + BLOCKS)
                    if not below(c, 2):
                        dve.wait_ge(out_stored[par], nth(c - 2, par))
                dve.scalar_tensor_tensor(out=x1[par][:, m, :], in0=acc[m][:, :], scalar=1.0 / 3.0,
                                         in1=x[par][:, m, :], op0=ALU.mult, op1=ALU.add
                                         ).then_inc(x1_done, 1)

            def low_x1(c, par, k):
                dve.wait_ge(x1_hi_done, c * KT + (k + 1))
                dve.tensor_tensor(x1_lo[:, k, :], x1[par][:, k, :], x1_hi[:, k, :].bitcast(F32),
                                  ALU.subtract).then_inc(x1_lo_done, 1)

            def output(c, par):
                dve.wait_ge(h_done, c * STEPS + STEPS)
                dve.tensor_tensor(x1[par][:, :, :], x1[par][:, :, :], h[par][:, :, :], ALU.add
                                  ).then_inc(out_done, 1)

            def split_h(q, r, par):
                if not (known(q, CHUNKS - 1) and r == STEPS - 1):
                    cols = slice(r * BATCH, (r + 1) * BATCH)
                    parts = [h_part[n][r % 2][:, :, :] for n in range(2)]
                    dve.wait_ge(h_done, q * STEPS + (r + 1))
                    dve.tensor_scalar(parts[0], h[par][:, :, cols], SCALE, None, ALU.mult
                                      ).then_inc(part_done[0], 1)
                    dve.wait_ge(part_done[0], q * STEPS + (r + 1))
                    dve.scalar_tensor_tensor(out=parts[1], in0=h[par][:, :, cols], scalar=SCALE,
                                             in1=parts[0], op0=ALU.mult, op1=ALU.subtract
                                             ).then_inc(part_done[1], 1)

            def split_wh():
                dve.wait_ge(small_loaded, 16)
                wh = small[:, WH:WH + KT * DIM]
                dve.tensor_scalar(wh_part[0][:, :], wh, 1.0 / SCALE, None, ALU.mult).then_inc(wh_step, 1)
                dve.wait_ge(wh_step, 1)
                dve.scalar_tensor_tensor(out=wh_rest[:, :], in0=wh, scalar=1.0 / SCALE,
                                         in1=wh_part[0][:, :], op0=ALU.mult, op1=ALU.subtract
                                         ).then_inc(wh_step, 1)
                dve.wait_ge(wh_step, 2)
                dve.tensor_copy(wh_part[1][:, :], wh_rest[:, :]).then_inc(wh_step, 1)
                dve.wait_ge(wh_step, 3)
                dve.tensor_tensor(wh_rest[:, :], wh_rest[:, :], wh_part[1][:, :], ALU.subtract
                                  ).then_inc(wh_step, 1)
                dve.wait_ge(wh_step, 4)
                dve.tensor_copy(wh_part[2][:, :], wh_rest[:, :]).then_inc(wh_step, 1)

            def split_bias():
                dve.memset(b_rows[:, :], 0.0).then_inc(b_step, 1)
                dve.memset(ones[:, :], 1.0).then_inc(b_step, 1)
                dve.wait_ge(b_loaded, 16)
                for n in range(3):
                    dve.tensor_copy(b_part[n][:, :], b_raw[:, :]).then_inc(b_step, 1)
                    dve.wait_ge(b_step, 3 + 2 * n)
                    if n < 2:
                        dve.tensor_tensor(b_raw[:, :], b_raw[:, :], b_part[n][:, :], ALU.subtract
                                          ).then_inc(b_step, 1)
                        dve.wait_ge(b_step, 4 + 2 * n)
                for n in range(3):
                    dve.tensor_copy(b_rows[32 * n:32 * n + 1, :], b_part[n][32 * n:32 * n + 1, :]
                                    ).then_inc(b_step, 1)

            def prologue():
                dve.wait_ge(t_bias_done, 1)
                dve.tensor_copy(t_bias[:, :], route[0:BATCH, 0:EXPERTS]).then_inc(t_bias_copied, 1)
                low_x(0, 0)
                low_w(0)
                low_w(1)
                dve.wait_ge(rw_hi_done, 1)
                dve.tensor_tensor(rw_pad[:, :, EXPERTS:2 * EXPERTS],
                                  small[:, RW:RW + KT * EXPERTS].rearrange("p (k e) -> p k e", k=KT),
                                  rw_pad[:, :, 0:EXPERTS].bitcast(F32), ALU.subtract
                                  ).then_inc(rw_lo_done, 1)

            def body(c, par, new, one, two, nxt):
                for i in range(STEPS):
                    steps = steps_of(c, i, one, two)
                    if i == 0 and one:
                        routed_product(c - 1, EXPERTS - 1, 1 - par)
                    if i == 2 and one:
                        residual(c - 1, 1 - par, 0)
                    if i > 8 and new:
                        routed_product(c, i - 9, par)
                    for back, r in steps[:1]:
                        split_h(c - back, r, par if back == 2 else 1 - par)
                    if i == 0 and one:
                        low(c - 1, BLOCKS - 1)
                    if i == 2 and one:
                        residual(c - 1, 1 - par, 1)
                        low_x1(c - 1, 1 - par, 0)
                        low_x1(c - 1, 1 - par, 1)
                    if i in (2, 4, 6, 8) and new:
                        shared_product(c, i // 2 - 1)
                    if i in (1, 3, 5, 7) and new:
                        half_silu(c, i // 2)
                    if i in (3, 4, 6, 8) and new:
                        low(c, {3: 0, 4: 1, 6: 2, 8: 3}[i])
                    if i > 8 and new:
                        low(c, SHARED + i - 9)
                    for back, r in steps[1:]:
                        split_h(c - back, r, par if back == 2 else 1 - par)
                    if i == 3 and two:
                        output(c - 2, par)
                    if i == 4 and nxt:
                        low_x(c + 1, 1 - par)
                    if known(c, 0):
                        if i == 2:
                            logits(0)
                        if i in (3, 4, 5):
                            for piece in {3: (0, 1, 2), 4: (3, 4), 5: (5, 6)}[i]:
                                routing(0, 0, piece)
                        if i == 9:
                            split_bias()
                        if i == 10:
                            split_wh()
                    if i == 6 and nxt:
                        logits(c + 1)
                    if i >= 8 and i < 15 and nxt:
                        routing(c + 1, 1 - par, i - 8)

            schedule(dve, prologue, body)


def kernel(x, cond_1024, L0_cond_router_w, L0_cond_router_t_w, L0_cond_router_bias, L0_cond_sw1,
           L0_cond_sw3, L0_cond_sw2, L0_cond_rw1, L0_cond_rw2, L1_cond_Wx, L1_cond_Wh, L1_cond_b):
    import numpy as np
    import concourse.bacc as bacc
    from concourse.bass_utils import run_bass_kernel_spmd

    def rows(a):
        a = np.asarray(a).reshape(KT, P, -1)
        return a.transpose(1, 0, 2).reshape(P, -1)

    def cols(a):
        return rows(np.asarray(a).T)

    x_np = np.asarray(x).reshape(BATCH, CHUNKS, STEPS, KT, P).transpose(1, 4, 3, 2, 0)
    x_np = np.ascontiguousarray(x_np).reshape(CHUNKS * P, KT * TOK)
    sw2, rw1, rw2 = np.asarray(L0_cond_sw2), np.asarray(L0_cond_rw1), np.asarray(L0_cond_rw2)
    w_np = np.concatenate([
        cols(L0_cond_sw1), cols(L0_cond_sw3),
        sw2.T.reshape(SHARED, P, DIM).transpose(1, 0, 2).reshape(P, -1),
        rw1.reshape(EXPERTS, P, KT, P).transpose(3, 0, 2, 1).reshape(P, -1),
        rw2.transpose(2, 0, 1).reshape(P, -1),
        rows(L1_cond_Wx)], axis=1)
    bias = np.broadcast_to(np.asarray(L0_cond_router_bias)[None, :], (P, EXPERTS))
    rank = np.broadcast_to(np.arange(EXPERTS, 0, -1, dtype=np.float32)[None, :], (P, EXPERTS))
    s_np = np.concatenate([rows(L1_cond_Wh), cols(cond_1024), cols(L0_cond_router_w), cols(L0_cond_router_t_w),
                           bias, rank], axis=1)

    nc = bacc.Bacc("TRN2", target_bir_lowering=False, num_devices=1)
    arrays = {"x_in": x_np, "w_in": np.ascontiguousarray(w_np), "s_in": np.ascontiguousarray(s_np),
              "b_in": np.asarray(L1_cond_b).reshape(1, DIM)}
    ins = [nc.dram_tensor(n, a.shape, F32, kind="ExternalInput").ap() for n, a in arrays.items()]
    scratch = nc.dram_tensor("scratch", (2 * EXPERTS, TOK), F32, kind="Internal").ap()
    out = nc.dram_tensor("out", (CHUNKS * P, KT * TOK), F32, kind="ExternalOutput").ap()
    moe_rnn(nc, *ins, scratch, out)
    got = run_bass_kernel_spmd(nc, [arrays], core_ids=[0]).results[0]["out"]
    got = got.reshape(CHUNKS, P, KT, STEPS, BATCH).transpose(4, 0, 3, 2, 1)
    return np.ascontiguousarray(got).reshape(BATCH, TIME, DIM)
```

```python
from contextlib import ExitStack

import concourse.bass as bass
from concourse import mybir

F32 = mybir.dt.float32
F32R = mybir.dt.float32r
BF16 = mybir.dt.bfloat16
F16 = mybir.dt.float16
ALU = mybir.AluOpType
ACT = mybir.ActivationFunctionType
AX = mybir.AxisListType

P = 128
BATCH, TIME, DIM = 32, 256, 256
EXPERTS = 8
HIDDEN_SHARED = 512
STEPS = 16
TOK = STEPS * BATCH
CHUNKS = TIME // STEPS
KT = DIM // P
SHARED = HIDDEN_SHARED // P
BLOCKS = SHARED + EXPERTS
TILES = 2 * SHARED + EXPERTS
LAG = 4
EPS = 1e-9
H_SCALE = 2.0 ** 12
W_SCALE = 2.0 ** 13
PRODUCTS = [[0, 1], [0]]
EXPONENT = 0x7F800000
BIAS_ROWS = 96
RING = [0, 1, 2] * 5 + [1]
W1, W3, W2, R1, R2, WX = 0, 1024, 2048, 3072, 5120, 7168
W_COLS = 7680
GROUP = 1024
GROUPS = [(a, min(a + GROUP, W_COLS)) for a in range(0, W_COLS, GROUP)]
WH, COND, RW, RT, RB, RANK = 0, 512, 576, 592, 608, 616
S_COLS = 624
DOWN = {0: [(10, (0, 1), 1)], 1: [(11, (0, 1), 1)],
        4: [(0, (0,), 0)], 5: [(0, (1,), 0)], 6: [(1, (0,), 0)], 7: [(1, (1,), 0)],
        8: [(2, (0, 1), 0)], 9: [(3, (0, 1), 0)],
        **{10 + e: [(4 + e, (0, 1), 0)] for e in range(6)}}
ROUTER_OPS = 27
FIRST_GATES = 2
SCALE_OPS, WH_OPS, B_OPS = 5, 5, 11
LOGIT_OPS = 3


def moe_rnn(nc, x_in, w_in, s_in, b_in, scratch, out):
    with ExitStack() as ctx:
        def sb(name, shape, dt=F32):
            return ctx.enter_context(nc.sbuf_tensor(name, shape, dt))

        def pb(name, shape):
            return ctx.enter_context(nc.psum_tensor(name, shape, F32))

        def sem(name):
            return ctx.enter_context(nc.semaphore(name))

        w_raw = sb("w_raw", [P, W_COLS - 4 * GROUP])
        w_hi = sb("w_hi", [P, W_COLS], F32R)
        w_lo = sb("w_lo", [P, W_COLS], F32R)
        small = sb("small", [P, S_COLS])
        x = [sb(f"x{p}", [P, KT, TOK]) for p in range(2)]
        x_hi = [sb(f"x_hi{p}", [P, KT, TOK], F32R) for p in range(2)]
        x_lo = [sb(f"x_lo{p}", [P, KT, TOK], F32R) for p in range(2)]
        x1 = [sb(f"x1_{p}", [P, KT, TOK]) for p in range(2)]
        x1_hi = sb("x1_hi", [P, KT, TOK], F32R)
        x1_lo = sb("x1_lo", [P, KT, TOK], F32R)
        h = [sb(f"h{p}", [P, KT, TOK]) for p in range(2)]
        h_part = [[sb(f"h_part{n}_{s}", [P, KT, BATCH], F16) for s in range(2)] for n in range(2)]
        wh_part = [sb(f"wh_part{n}", [P, KT * DIM], F16) for n in range(2)]
        zero = sb("zero", [P, 1])
        row_max = sb("row_max", [P, 1])
        wh_max = sb("wh_max", [P, 1])
        wh_inv = sb("wh_inv", [P, 1])
        x_factor = sb("x_factor", [P, 1])
        tanh_scale = sb("tanh_scale", [P, 1])
        wh_rest = sb("wh_rest", [P, KT * DIM])
        b_raw = sb("b_raw", [BIAS_ROWS, DIM])
        b_part = [sb(f"b_part{n}", [BIAS_ROWS, DIM], BF16) for n in range(3)]
        b_rows = sb("b_rows", [BIAS_ROWS, DIM], BF16)
        ones = sb("ones", [BIAS_ROWS, TOK], BF16)
        gate_bc = [sb(f"gate_bc{p}", [P, EXPERTS, TOK]) for p in range(2)]
        g = [sb(f"g{i}", [P, TOK]) for i in range(2)]
        u = sb("u", [P, TOK])
        hs = [sb(f"hs{i}", [P, TOK]) for i in range(2)]
        hs_hi = [sb(f"hs_hi{i}", [P, TOK], F32R) for i in range(3)]
        hs_lo = [sb(f"hs_lo{i}", [P, TOK], F32R) for i in range(3)]
        rw_pad = sb("rw_pad", [P, KT, P], F32R)
        t_bias = sb("t_bias", [BATCH, EXPERTS])
        route_t = sb("route_t", [BATCH, STEPS, 32])
        logit = sb("logit", [BATCH, STEPS, EXPERTS])
        score = sb("score", [BATCH, STEPS, EXPERTS])
        sel = sb("sel", [BATCH, STEPS, EXPERTS])
        hit = sb("hit", [BATCH, STEPS, EXPERTS])
        first = sb("first", [BATCH, STEPS, EXPERTS])
        second = sb("second", [BATCH, STEPS, EXPERTS])
        top = sb("top", [BATCH, STEPS])
        den = sb("den", [BATCH, STEPS])
        inv = sb("inv", [BATCH, STEPS])
        big = sb("big", [BATCH, STEPS])
        comb = sb("comb", [BATCH, STEPS, 32])
        comb_t = [sb(f"comb_t{p}", [32, TOK]) for p in range(2)]
        gelu_probe = sb("gelu_probe", [BATCH, 1])

        up = [pb(f"up{i}", [P, TOK]) for i in range(3)]
        acc = [pb(f"acc{m}", [P, TOK]) for m in range(KT)]
        rec = pb("rec", [P, KT, TOK])
        route = pb("route", [P, 512])

        small_loaded = sem("small_loaded")
        w_loaded = [sem(f"w_loaded{i}") for i in range(len(GROUPS))]
        x_loaded = [sem(f"x_loaded{p}") for p in range(2)]
        comb_stored = sem("comb_stored")
        gate_loaded = [sem(f"gate_loaded{p}") for p in range(2)]
        first_gates_loaded = sem("first_gates_loaded")
        out_stored = [sem(f"out_stored{p}") for p in range(2)]
        w_hi_done = sem("w_hi_done")
        w_lo_done = sem("w_lo_done")
        w_rest_done = sem("w_rest_done")
        rw_cleared = sem("rw_cleared")
        rw_hi_done = sem("rw_hi_done")
        rw_lo_done = sem("rw_lo_done")
        zero_set = sem("zero_set")
        comb_cleared = sem("comb_cleared")
        x_hi_done = sem("x_hi_done")
        x_lo_done = sem("x_lo_done")
        t_bias_done = sem("t_bias_done")
        t_bias_copied = sem("t_bias_copied")
        route_done = sem("route_done")
        score_done = sem("score_done")
        router_step = sem("router_step")
        up_done = sem("up_done")
        down_done = sem("down_done")
        act_done = sem("act_done")
        u_done = sem("u_done")
        hs_done = sem("hs_done")
        hi_done = sem("hi_done")
        lo_done = sem("lo_done")
        x1_done = sem("x1_done")
        x1_hi_done = sem("x1_hi_done")
        x1_lo_done = sem("x1_lo_done")
        wx_done = sem("wx_done")
        rec_done = sem("rec_done")
        h_done = sem("h_done")
        part_done = [sem(f"part{n}_done") for n in range(2)]
        b_loaded = sem("b_loaded")
        row_max_done = sem("row_max_done")
        wh_max_done = sem("wh_max_done")
        scale_step = sem("scale_step")
        wx_scaled = sem("wx_scaled")
        wh_step = sem("wh_step")
        b_step = sem("b_step")
        out_done = sem("out_done")

        block = ctx.enter_context(nc.Block())

        def schedule(eng, prologue, body):
            prologue()
            body(0, 0, new=True, one=False, two=False, nxt=True)
            body(1, 1, new=True, one=True, two=False, nxt=True)
            body(2, 0, new=True, one=True, two=True, nxt=True)
            with eng.Fori(1, CHUNKS // 2 - 1) as pair:
                body(pair * 2 + 1, 1, new=True, one=True, two=True, nxt=True)
                body(pair * 2 + 2, 0, new=True, one=True, two=True, nxt=True)
            body(CHUNKS - 1, 1, new=True, one=True, two=True, nxt=False)
            body(CHUNKS, 0, new=False, one=True, two=True, nxt=False)
            body(CHUNKS + 1, 1, new=False, one=False, two=True, nxt=False)

        def steps_of(c, i, one, two):
            if known(c, CHUNKS - 1):
                if i < LAG:
                    return [(2, STEPS - LAG + i)]
                if i < 8:
                    return [(1, i - LAG)]
                r = i - LAG + (i - 7) // 2
                return [(1, r)] if i % 2 else [(1, r), (1, r + 1)]
            if i < LAG:
                return [(2, STEPS - LAG + i)] if two and not known(c, CHUNKS) else []
            return [(1, i - LAG)] if one else []

        def raw(n):
            a, b = GROUPS[n]
            if R1 <= a < WX:
                return gate_bc[1][:, :, :].rearrange("p e n -> p (e n)")[:, a - R1:b - R1]
            return w_raw[:, a:b] if a < R1 else w_raw[:, a - 4 * GROUP:b - 4 * GROUP]

        def known(c, n):
            return isinstance(c, int) and c == n

        def below(c, n):
            return isinstance(c, int) and c < n

        def nth(c, par):
            return c * 8 + (16 - 8 * par)

        @block.sync
        def _(sp):
            def load_x(c, par):
                sp.dma_start(x[par][:, :, :], x_in[bass.ts(c, P), :].rearrange("p (k n) -> p k n", k=KT)
                             ).then_inc(x_loaded[par], 16)

            def load_w(n):
                a, b = GROUPS[n]
                sp.dma_start(raw(n), w_in[:, a:b]).then_inc(w_loaded[n], 16)

            def gates(c, par):
                sp.wait_ge(router_step, c * ROUTER_OPS + ROUTER_OPS)
                if not below(c, 2):
                    sp.wait_ge(gate_loaded[par], nth(c - 2, par))
                rows = scratch[par * EXPERTS:(par + 1) * EXPERTS, :]
                sp.dma_start(rows, comb_t[par][0:EXPERTS, :]).then_inc(comb_stored, 16)
                sp.wait_ge(comb_stored, c * 16 + 16)
                if not below(c, 2):
                    sp.wait_ge(hs_done, c * BLOCKS - BLOCKS)
                if known(c, 1):
                    sp.wait_ge(w_rest_done, 5)
                flat = rows.rearrange("(o e) n -> o (e n)", o=1)
                into = gate_bc[par][:, :, :].rearrange("p e n -> p (e n)")
                early = FIRST_GATES * TOK if known(c, 0) else 0
                if early:
                    sp.dma_start(into[:, 0:early], flat[:, 0:early].broadcast_to([P, early])
                                 ).then_inc(first_gates_loaded, 16)
                sp.dma_start(into[:, early:], flat[:, early:].broadcast_to([P, EXPERTS * TOK - early])
                             ).then_inc(gate_loaded[par], 16)

            def prologue():
                load_x(0, 0)
                load_w(0)
                load_w(1)
                load_x(1, 1)
                for n in range(2, len(GROUPS)):
                    load_w(n)

            def body(c, par, new, one, two, nxt):
                if known(c, 0):
                    gates(0, 0)
                if nxt and not known(c, 0):
                    sp.wait_ge(x1_done, c * KT)
                    load_x(c + 1, 1 - par)
                if two:
                    sp.wait_ge(out_done, c - 1)
                    sp.dma_start(out[bass.ts(c - 2, P), :].rearrange("p (k n) -> p k n", k=KT),
                                 x1[par][:, :, :]).then_inc(out_stored[par], 16)
                if nxt:
                    gates(c + 1, 1 - par)

            schedule(sp, prologue, body)
            for par in range(2):
                sp.wait_ge(out_stored[par], 16 * (CHUNKS // 2))

        @block.tensor
        def _(pe):
            def three(dst, col, hi, lo, start, stop, inc=None):
                wh, wl = w_hi[:, col:col + P], w_lo[:, col:col + P]
                pe.matmul(dst, wh, hi, start=start, stop=False, skip_group_check=True)
                pe.matmul(dst, wh, lo, start=False, stop=False, skip_group_check=True)
                mm = pe.matmul(dst, wl, hi, start=False, stop=stop, skip_group_check=True)
                if inc is not None:
                    mm.then_inc(inc, 1)

            def router(c, par):
                if known(c, 0):
                    pe.wait_ge(rw_lo_done, 1)
                    pe.wait_ge(t_bias_copied, 1)
                else:
                    pe.wait_ge(router_step, c * ROUTER_OPS + (1 - ROUTER_OPS))
                pe.wait_ge(x_lo_done, c + 1)
                for k in range(KT):
                    for part in (x_hi, x_lo):
                        mm = pe.matmul(route[:, :], rw_pad[:, k, :], part[par][:, k, :],
                                       start=(k == 0 and part is x_hi),
                                       stop=(k == KT - 1 and part is x_lo))
                mm.then_inc(route_done, 1)

            def recur(q, r):
                cols = slice(r * BATCH, (r + 1) * BATCH)
                if known(q, 0) and r == 0:
                    pe.wait_ge(wh_step, 1)
                    for m in range(KT):
                        for k in range(KT):
                            mm = pe.matmul(rec[:, m, cols],
                                           small[:, WH + k * DIM + m * P:WH + k * DIM + (m + 1) * P],
                                           small[:, COND + k * BATCH:COND + (k + 1) * BATCH],
                                           start=False, stop=(k == KT - 1), skip_group_check=True)
                    mm.then_inc(rec_done, 1)
                    return
                if known(q, 0) and r == 1:
                    pe.wait_ge(wh_step, WH_OPS)
                for n in range(2):
                    pe.wait_ge(part_done[n], q * STEPS + r)
                    for m in range(KT):
                        for k in range(KT):
                            for w in PRODUCTS[n]:
                                mm = pe.matmul(rec[:, m, cols],
                                               wh_part[w][:, k * DIM + m * P:k * DIM + (m + 1) * P],
                                               h_part[n][(r - 1) % 2][:, k, :], start=False,
                                               stop=(n == 1 and k == KT - 1 and w == PRODUCTS[1][-1]),
                                               skip_group_check=True)
                mm.then_inc(rec_done, 1)

            def input_part(q):
                if known(q, 0):
                    pe.wait_ge(b_step, B_OPS)
                else:
                    pe.wait_ge(h_done, q * STEPS)
                for m in range(KT):
                    pe.matmul(rec[:, m, :], b_rows[:, m * P:(m + 1) * P], ones[:, :],
                              start=True, stop=False, skip_group_check=True)
                for k in range(KT):
                    pe.wait_ge(x1_lo_done, q * KT + (k + 1))
                    for m in range(KT):
                        last = k == KT - 1 and m == KT - 1
                        three(rec[:, m, :], WX + k * DIM + m * P, x1_hi[:, k, :], x1_lo[:, k, :],
                              False, False, wx_done if last else None)

            def up_waits(c, i):
                back, prev = 0, i - 1
                while RING[prev % TILES] != RING[i]:
                    prev -= 1
                if prev < 0:
                    back, prev = 1, prev + TILES
                if not (known(c, 0) and back):
                    if prev >= 2 * SHARED:
                        pe.wait_ge(act_done, c * BLOCKS + (prev - SHARED + 1 - back * BLOCKS))
                    elif prev % 2:
                        pe.wait_ge(hs_done, c * BLOCKS + (prev // 2 + 1 - back * BLOCKS))
                    else:
                        pe.wait_ge(u_done, c * SHARED + (prev // 2 + 1 - back * SHARED))
                if i == 0:
                    pe.wait_ge(x_lo_done, c + 1)
                if known(c, 0):
                    if i < 2:
                        pe.wait_ge(w_lo_done, i + 1)
                    if i in (8, 12):
                        pe.wait_ge(w_rest_done, i // 4)

            def up_tile(c, i, par, ks):
                if ks[0] == 0:
                    up_waits(c, i)
                for k in ks:
                    if i < 2 * SHARED:
                        col = (W3 if i % 2 else W1) + k * HIDDEN_SHARED + (i // 2) * P
                    else:
                        col = R1 + (i - 2 * SHARED) * DIM + k * P
                    three(up[RING[i]][:, :], col, x_hi[par][:, k, :], x_lo[par][:, k, :],
                          k == 0, k == KT - 1, up_done if k == KT - 1 else None)

            def down(c, b, ms):
                if ms[0] == 0:
                    pe.wait_ge(lo_done, c * BLOCKS + (b + 1))
                    if b == 0 and not known(c, 0):
                        pe.wait_ge(x1_done, c * KT)
                    if known(c, 0) and b in (0, 4, 8):
                        pe.wait_ge(w_rest_done, {0: 1, 4: 4, 8: 5}[b])
                for m in ms:
                    col = (W2 + b * DIM if b < SHARED else R2 + (b - SHARED) * DIM) + m * P
                    three(acc[m][:, :], col, hs_hi[b % 3][:, :], hs_lo[b % 3][:, :],
                          b == 0, b == BLOCKS - 1, down_done if m == KT - 1 else None)

            def prologue():
                pe.wait_ge(small_loaded, 16)
                for k in range(KT):
                    mm = pe.matmul(route[0:BATCH, 0:EXPERTS],
                                   small[:, COND + k * BATCH:COND + (k + 1) * BATCH],
                                   small[:, RT + k * EXPERTS:RT + (k + 1) * EXPERTS],
                                   start=(k == 0), stop=(k == KT - 1))
                mm.then_inc(t_bias_done, 1)
                router(0, 0)

            def body(c, par, new, one, two, nxt):
                for i in range(STEPS):
                    steps = steps_of(c, i, one, two)
                    for back, r in steps[:1]:
                        recur(c - back, r)
                    if new and i == 3:
                        up_tile(c, 3, par, (1,))
                    elif new:
                        up_tile(c, i, par, (0, 1))
                    if new and i == 2:
                        up_tile(c, 3, par, (0,))
                    for back, r in steps[1:]:
                        recur(c - back, r)
                    if i == LAG + 2 and nxt:
                        router(c + 1, 1 - par)
                    for b, ms, back in DOWN.get(i, []):
                        if back and one:
                            down(c - 1, b, ms)
                        if not back and new:
                            down(c, b, ms)
                    if i == LAG - 1 and one:
                        if known(c, 1):
                            pe.wait_ge(w_rest_done, 6)
                        input_part(c - 1)

            schedule(pe, prologue, body)

        @block.scalar
        def _(act):
            def split_w(n):
                a, b = GROUPS[n]
                act.wait_ge(w_loaded[n], 16)
                if n == len(GROUPS) - 1:
                    act.wait_ge(wx_scaled, 1)
                act.copy(w_hi[:, a:b], raw(n)).then_inc(w_hi_done, 1)

            def split_x(c, par):
                act.wait_ge(x_loaded[par], nth(c, par))
                act.copy(x_hi[par][:, :, :], x[par][:, :, :]).then_inc(x_hi_done, 1)

            def squash(c, b):
                tile = 2 * b if b < SHARED else b + SHARED
                act.wait_ge(up_done, c * TILES + (tile + 1))
                if not (known(c, 0) and b < 2):
                    act.wait_ge(hs_done, c * BLOCKS + (b - 1))
                if b < SHARED:
                    ins = act.activation(g[b % 2][:, :], up[RING[tile]][:, :], ACT.Tanh, scale=0.5)
                else:
                    ins = act.activation(g[b % 2][:, :], up[RING[tile]][:, :], ACT.Gelu)
                ins.then_inc(act_done, 1)

            def high(c, b):
                act.wait_ge(hs_done, c * BLOCKS + (b + 1))
                if not (known(c, 0) and b < 3):
                    act.wait_ge(down_done, c * BLOCKS + (b - 2))
                act.copy(hs_hi[b % 3][:, :], hs[b % 2][:, :]).then_inc(hi_done, 1)

            def recur(q, r, par):
                if r == 0 and not below(q, 2):
                    act.wait_ge(out_done, q - 1)
                act.wait_ge(rec_done, q * STEPS + (r + 1))
                if known(q, 0) and r == 0:
                    act.wait_ge(scale_step, SCALE_OPS)
                cols = slice(r * BATCH, (r + 1) * BATCH)
                act.activation(h[par][:, :, cols], rec[:, :, cols], ACT.Tanh, scale=tanh_scale[:, :]
                               ).then_inc(h_done, 1)

            def sigmoid(c):
                act.wait_ge(router_step, c * ROUTER_OPS + LOGIT_OPS)
                act.activation(score[:, :, :], logit[:, :, :], ACT.Sigmoid).then_inc(score_done, 1)

            def load_gelu(c):
                act.wait_ge(score_done, c + 1)
                act.activation(gelu_probe[:, :], score[:, 0, 0:1], ACT.Gelu)

            def prologue():
                act.dma_start(small[:, :], s_in[:, :]).then_inc(small_loaded, 16)
                act.dma_start(b_raw[:, :], b_in.broadcast_to([BIAS_ROWS, DIM])).then_inc(b_loaded, 16)
                act.wait_ge(zero_set, 1)
                act.activation(gelu_probe[:, :], zero[0:BATCH, :], ACT.Gelu)
                act.wait_ge(rw_cleared, 1)
                act.wait_ge(small_loaded, 16)
                act.copy(rw_pad[:, :, 0:EXPERTS],
                         small[:, RW:RW + KT * EXPERTS].rearrange("p (k e) -> p k e", k=KT)
                         ).then_inc(rw_hi_done, 1)
                split_x(0, 0)
                split_w(0)
                split_w(1)
                sigmoid(0)

            def body(c, par, new, one, two, nxt):
                for i in range(STEPS):
                    if i == 0 and one:
                        squash(c - 1, BLOCKS - 1)
                    if new and i in (1, 3, 5, 7):
                        squash(c, i // 2)
                    if new and i > 8:
                        squash(c, SHARED + i - 9)
                    steps = steps_of(c, i, one, two)
                    for back, r in steps[:1]:
                        recur(c - back, r, par if back == 2 else 1 - par)
                    if i == 0 and one:
                        high(c - 1, BLOCKS - 1)
                    if i == 2 and one:
                        for k in range(KT):
                            act.wait_ge(x1_done, c * KT - KT + (k + 1))
                            if not known(c, 1):
                                act.wait_ge(wx_done, c - 1)
                            act.copy(x1_hi[:, k, :], x1[1 - par][:, k, :]).then_inc(x1_hi_done, 1)
                    if new and i in (3, 4, 6, 8):
                        high(c, {3: 0, 4: 1, 6: 2, 8: 3}[i])
                    if new and i > 8:
                        high(c, SHARED + i - 9)
                    for back, r in steps[1:]:
                        recur(c - back, r, par if back == 2 else 1 - par)
                    if i == 4 and known(c, 0):
                        split_x(1, 1)
                    if known(c, 0):
                        if i in (0, 2, 3, 5, 6, 14):
                            split_w({0: 2, 2: 3, 3: 4, 5: 5, 6: 6, 14: 7}[i])
                    if i == 7 and nxt:
                        sigmoid(c + 1)
                    if i == 8 and nxt:
                        load_gelu(c + 1)

            schedule(act, prologue, body)

        @block.gpsimd
        def _(pool):
            pool.memset(rw_pad[:, :, :].bitcast(F32), 0.0).then_inc(rw_cleared, 1)
            pool.memset(comb[:, :, :], 0.0).then_inc(comb_cleared, 1)
            pool.memset(zero[:, :], 0.0).then_inc(zero_set, 1)
            pool.memset(b_rows[:, :], 0.0).then_inc(b_step, 1)
            pool.memset(ones[:, :], 1.0).then_inc(b_step, 1)

            def low_w(n):
                a, b = GROUPS[n]
                pool.wait_ge(w_hi_done, n + 1)
                pool.tensor_tensor(w_lo[:, a:b], raw(n), w_hi[:, a:b].bitcast(F32), ALU.subtract
                                   ).then_inc(w_rest_done, 1)

            zeros = zero[:, :].rearrange("p (k n) -> p k n", k=1).broadcast_to([P, KT, TOK])

            def split_x(c, par):
                pool.wait_ge(x_loaded[par], nth(c, par))
                pool.wait_ge(up_done, c * TILES - TILES)
                pool.tensor_tensor(x_hi[par][:, :, :], x[par][:, :, :], zeros, ALU.add
                                   ).then_inc(x_hi_done, 1)
                pool.wait_ge(x_hi_done, c + 1)
                pool.tensor_tensor(x_lo[par][:, :, :], x[par][:, :, :], x_hi[par][:, :, :].bitcast(F32),
                                   ALU.subtract).then_inc(x_lo_done, 1)

            def prologue():
                pool.wait_ge(zero_set, 1)
                low_w(2)
                pool.wait_ge(row_max_done, 1)
                nc.gpsimd.partition_all_reduce(wh_max[:, :], row_max[:, :], P, bass.bass_isa.ReduceOp.max
                                               ).then_inc(wh_max_done, 1)
                for n in range(3, len(GROUPS) - 1):
                    low_w(n)
                pool.wait_ge(scale_step, SCALE_OPS)
                pool.wait_ge(w_loaded[-1], 16)
                pool.tensor_scalar(raw(len(GROUPS) - 1), raw(len(GROUPS) - 1), x_factor[:, :], None, ALU.mult
                                   ).then_inc(wx_scaled, 1)
                wh = small[:, WH:WH + KT * DIM]
                pool.tensor_scalar(wh, wh, x_factor[:, :], None, ALU.mult).then_inc(wh_step, 1)
                pool.wait_ge(b_loaded, 16)
                pool.tensor_scalar(b_raw[:, :], b_raw[:, :], x_factor[0:BIAS_ROWS, :], None, ALU.mult
                                   ).then_inc(b_step, 1)
                pool.wait_ge(wh_step, 1)
                pool.tensor_scalar(wh_rest[:, :], wh, 1.0 / H_SCALE, None, ALU.mult).then_inc(wh_step, 1)
                pool.wait_ge(wh_step, 2)
                pool.tensor_copy(wh_part[0][:, :], wh_rest[:, :]).then_inc(wh_step, 1)
                pool.wait_ge(wh_step, 3)
                pool.tensor_tensor(wh_rest[:, :], wh_rest[:, :], wh_part[0][:, :], ALU.subtract
                                   ).then_inc(wh_step, 1)
                pool.wait_ge(wh_step, 4)
                pool.tensor_copy(wh_part[1][:, :], wh_rest[:, :]).then_inc(wh_step, 1)
                for n in range(3):
                    pool.wait_ge(b_step, 3 + 2 * n)
                    pool.tensor_copy(b_part[n][:, :], b_raw[:, :]).then_inc(b_step, 1)
                    if n < 2:
                        pool.wait_ge(b_step, 4 + 2 * n)
                        pool.tensor_tensor(b_raw[:, :], b_raw[:, :], b_part[n][:, :], ALU.subtract
                                           ).then_inc(b_step, 1)
                pool.wait_ge(b_step, 8)
                for n in range(3):
                    if n:
                        pool.wait_ge(b_step, 8 + n)
                    pool.tensor_copy(b_rows[32 * n:32 * n + 1, :], b_part[n][32 * n:32 * n + 1, :]
                                     ).then_inc(b_step, 1)
                pool.wait_ge(b_step, B_OPS)
                low_w(len(GROUPS) - 1)

            def body(c, par, new, one, two, nxt):
                if nxt and not known(c, 0):
                    split_x(c + 1, 1 - par)

            schedule(pool, prologue, body)

        @block.vector
        def _(dve):
            def low_w(n):
                a, b = GROUPS[n]
                dve.wait_ge(w_hi_done, n + 1)
                dve.tensor_tensor(w_lo[:, a:b], raw(n), w_hi[:, a:b].bitcast(F32), ALU.subtract
                                  ).then_inc(w_lo_done, 1)

            def low_x(c, par):
                dve.wait_ge(x_hi_done, c + 1)
                dve.tensor_tensor(x_lo[par][:, :, :], x[par][:, :, :], x_hi[par][:, :, :].bitcast(F32),
                                  ALU.subtract).then_inc(x_lo_done, 1)

            def half_silu(c, j):
                dve.wait_ge(act_done, c * BLOCKS + (j + 1))
                if j:
                    dve.wait_ge(hs_done, c * BLOCKS + j)
                dve.scalar_tensor_tensor(out=u[:, :], in0=g[j % 2][:, :], scalar=1.0,
                                         in1=up[RING[2 * j]][:, :], op0=ALU.add, op1=ALU.mult
                                         ).then_inc(u_done, 1)

            def shared_product(c, j):
                dve.wait_ge(u_done, c * SHARED + (j + 1))
                dve.wait_ge(up_done, c * TILES + (2 * j + 2))
                dve.scalar_tensor_tensor(out=hs[j % 2][:, :], in0=u[:, :], scalar=0.5,
                                         in1=up[RING[2 * j + 1]][:, :], op0=ALU.mult, op1=ALU.mult
                                         ).then_inc(hs_done, 1)

            def routed_product(c, e, par):
                b = SHARED + e
                if known(c, 0) and e == 0:
                    dve.wait_ge(first_gates_loaded, 16)
                if e == (FIRST_GATES if known(c, 0) else 0):
                    dve.wait_ge(gate_loaded[par], nth(c, par))
                dve.wait_ge(act_done, c * BLOCKS + (b + 1))
                dve.tensor_tensor(hs[b % 2][:, :], g[b % 2][:, :], gate_bc[par][:, e, :], ALU.mult
                                  ).then_inc(hs_done, 1)

            def low(c, b):
                dve.wait_ge(hi_done, c * BLOCKS + (b + 1))
                dve.tensor_tensor(hs_lo[b % 3][:, :], hs[b % 2][:, :], hs_hi[b % 3][:, :].bitcast(F32),
                                  ALU.subtract).then_inc(lo_done, 1)

            def each(a):
                return a.rearrange("p (t o) -> p t o", o=1).broadcast_to([BATCH, STEPS, EXPERTS])

            def per_expert(a):
                return a.rearrange("p (o e) -> p o e", o=1).broadcast_to([BATCH, STEPS, EXPERTS])

            def logits(c):
                base = c * ROUTER_OPS
                dve.wait_ge(route_done, c + 1)
                if known(c, 0):
                    dve.wait_ge(t_bias_copied, 1)
                dve.transpose(route_t[:, :, :].rearrange("p s r -> p (s r)"), route[0:32, :]
                              ).then_inc(router_step, 1)
                dve.wait_ge(router_step, base + 1)
                dve.tensor_tensor(logit[:, :, :], route_t[:, :, 0:EXPERTS],
                                  route_t[:, :, EXPERTS:2 * EXPERTS], ALU.add).then_inc(router_step, 1)
                dve.wait_ge(router_step, base + 2)
                dve.tensor_tensor(logit[:, :, :], logit[:, :, :], per_expert(t_bias[:, :]), ALU.add
                                  ).then_inc(router_step, 1)

            def selection(c):
                dve.wait_ge(score_done, c + 1)
                dve.tensor_tensor(sel[:, :, :], score[:, :, :],
                                  per_expert(small[0:BATCH, RB:RB + EXPERTS]), ALU.add
                                  ).then_inc(router_step, 1)

            def reach(c, n):
                base = c * ROUTER_OPS + n
                dve.wait_ge(router_step, base)
                dve.tensor_reduce(top[:, :], sel[:, :, :], AX.X, ALU.max).then_inc(router_step, 1)
                dve.wait_ge(router_step, base + 1)
                dve.tensor_tensor(hit[:, :, :], sel[:, :, :], each(top[:, :]), ALU.is_equal
                                  ).then_inc(router_step, 1)
                dve.wait_ge(router_step, base + 2)
                dve.tensor_tensor(hit[:, :, :], hit[:, :, :],
                                  per_expert(small[0:BATCH, RANK:RANK + EXPERTS]), ALU.mult
                                  ).then_inc(router_step, 1)

            def lowest(c, n, one):
                base = c * ROUTER_OPS + n
                dve.wait_ge(router_step, base)
                dve.tensor_reduce(top[:, :], hit[:, :, :], AX.X, ALU.max).then_inc(router_step, 1)
                dve.wait_ge(router_step, base + 1)
                dve.tensor_tensor(one[:, :, :], hit[:, :, :], each(top[:, :]), ALU.is_equal
                                  ).then_inc(router_step, 1)

            def strike_first(c):
                dve.wait_ge(router_step, c * ROUTER_OPS + 9)
                dve.scalar_tensor_tensor(out=sel[:, :, :], in0=first[:, :, :], scalar=-3.0e38,
                                         in1=sel[:, :, :], op0=ALU.mult, op1=ALU.add
                                         ).then_inc(router_step, 1)

            def picked_sum(c):
                base = c * ROUTER_OPS
                dve.wait_ge(router_step, base + 15)
                dve.tensor_tensor(second[:, :, :], first[:, :, :], second[:, :, :], ALU.add
                                  ).then_inc(router_step, 1)
                dve.wait_ge(router_step, base + 16)
                if known(c, 0):
                    dve.wait_ge(comb_cleared, 1)
                dve.tensor_tensor(comb[:, :, 0:EXPERTS], second[:, :, :], score[:, :, :], ALU.mult
                                  ).then_inc(router_step, 1)
                dve.wait_ge(router_step, base + 17)
                dve.tensor_reduce(den[:, :], comb[:, :, 0:EXPERTS], AX.X, ALU.add
                                  ).then_inc(router_step, 1)
                dve.wait_ge(router_step, base + 18)
                dve.tensor_scalar(inv[:, :], den[:, :], EPS, None, ALU.add).then_inc(router_step, 1)
                dve.tensor_scalar(big[:, :], den[:, :], EPS, None, ALU.is_gt).then_inc(router_step, 1)

            def factors(c):
                base = c * ROUTER_OPS
                dve.wait_ge(router_step, base + 19)
                dve.reciprocal(inv[:, :], inv[:, :]).then_inc(router_step, 1)
                dve.wait_ge(router_step, base + 21)
                dve.tensor_tensor(inv[:, :], inv[:, :], big[:, :], ALU.mult).then_inc(router_step, 1)
                dve.tensor_scalar(big[:, :], big[:, :], -0.5, 0.5, ALU.mult, ALU.add
                                  ).then_inc(router_step, 1)

            def combine(c, par):
                base = c * ROUTER_OPS
                dve.wait_ge(router_step, base + 23)
                dve.tensor_tensor(comb[:, :, 0:EXPERTS], comb[:, :, 0:EXPERTS], each(inv[:, :]), ALU.mult
                                  ).then_inc(router_step, 1)
                dve.tensor_tensor(second[:, :, :], second[:, :, :], each(big[:, :]), ALU.mult
                                  ).then_inc(router_step, 1)
                dve.wait_ge(router_step, base + 25)
                dve.tensor_tensor(comb[:, :, 0:EXPERTS], comb[:, :, 0:EXPERTS], second[:, :, :], ALU.add
                                  ).then_inc(router_step, 1)
                dve.wait_ge(router_step, base + 26)
                if not below(c, 2):
                    dve.wait_ge(comb_stored, c * 16 - 16)
                dve.transpose(comb_t[par][:, :], comb[:, :, :].rearrange("p t e -> p (t e)")
                              ).then_inc(router_step, 1)

            def routing(c, par, piece):
                if piece == 0:
                    selection(c)
                    reach(c, 4)
                if piece == 1:
                    lowest(c, 7, first)
                    strike_first(c)
                if piece == 2:
                    reach(c, 10)
                if piece == 3:
                    lowest(c, 13, second)
                if piece == 4:
                    picked_sum(c)
                if piece == 5:
                    factors(c)
                if piece == 6:
                    combine(c, par)

            def residual(c, par, m):
                if m == 0:
                    dve.wait_ge(down_done, c * BLOCKS + BLOCKS)
                    if not below(c, 2):
                        dve.wait_ge(out_stored[par], nth(c - 2, par))
                dve.scalar_tensor_tensor(out=x1[par][:, m, :], in0=acc[m][:, :], scalar=1.0 / 3.0,
                                         in1=x[par][:, m, :], op0=ALU.mult, op1=ALU.add
                                         ).then_inc(x1_done, 1)

            def low_x1(c, par, k):
                dve.wait_ge(x1_hi_done, c * KT + (k + 1))
                dve.tensor_tensor(x1_lo[:, k, :], x1[par][:, k, :], x1_hi[:, k, :].bitcast(F32),
                                  ALU.subtract).then_inc(x1_lo_done, 1)

            def output(c, par):
                dve.wait_ge(h_done, c * STEPS + STEPS)
                dve.tensor_tensor(x1[par][:, :, :], x1[par][:, :, :], h[par][:, :, :], ALU.add
                                  ).then_inc(out_done, 1)

            def split_h(q, r, par):
                if not (known(q, CHUNKS - 1) and r == STEPS - 1):
                    cols = slice(r * BATCH, (r + 1) * BATCH)
                    parts = [h_part[n][r % 2][:, :, :] for n in range(2)]
                    dve.wait_ge(h_done, q * STEPS + (r + 1))
                    dve.tensor_scalar(parts[0], h[par][:, :, cols], H_SCALE, None, ALU.mult
                                      ).then_inc(part_done[0], 1)
                    dve.wait_ge(part_done[0], q * STEPS + (r + 1))
                    dve.scalar_tensor_tensor(out=parts[1], in0=h[par][:, :, cols], scalar=H_SCALE,
                                             in1=parts[0], op0=ALU.mult, op1=ALU.subtract
                                             ).then_inc(part_done[1], 1)

            def factors_of_wh():
                i32 = mybir.dt.int32
                dve.wait_ge(wh_max_done, 1)
                dve.tensor_scalar(wh_max[:, :], wh_max[:, :], 2.0 ** -30, 2.0 ** 90, ALU.max, ALU.min
                                  ).then_inc(scale_step, 1)
                dve.wait_ge(scale_step, 1)
                dve.tensor_scalar(wh_max[:, :].bitcast(i32), wh_max[:, :].bitcast(i32), EXPONENT, None,
                                  ALU.bitwise_and).then_inc(scale_step, 1)
                dve.wait_ge(scale_step, 2)
                dve.tensor_scalar(wh_inv[:, :].bitcast(i32), wh_max[:, :].bitcast(i32), -1.0,
                                  float(254 << 23), ALU.mult, ALU.add).then_inc(scale_step, 1)
                dve.tensor_scalar(tanh_scale[:, :], wh_max[:, :], 1.0 / (H_SCALE * W_SCALE), None,
                                  ALU.mult).then_inc(scale_step, 1)
                dve.wait_ge(scale_step, 3)
                dve.tensor_scalar(x_factor[:, :], wh_inv[:, :], H_SCALE * W_SCALE, None, ALU.mult
                                  ).then_inc(scale_step, 1)

            def prologue():
                dve.wait_ge(t_bias_done, 1)
                dve.tensor_copy(t_bias[:, :], route[0:BATCH, 0:EXPERTS]).then_inc(t_bias_copied, 1)
                dve.wait_ge(rw_hi_done, 1)
                dve.tensor_tensor(rw_pad[:, :, EXPERTS:2 * EXPERTS],
                                  small[:, RW:RW + KT * EXPERTS].rearrange("p (k e) -> p k e", k=KT),
                                  rw_pad[:, :, 0:EXPERTS].bitcast(F32), ALU.subtract
                                  ).then_inc(rw_lo_done, 1)
                low_x(0, 0)
                low_w(0)
                logits(0)
                low_w(1)
                routing(0, 0, 0)
                dve.tensor_reduce(row_max[:, :], small[:, WH:WH + KT * DIM], AX.X, ALU.max,
                                  apply_absolute_value=True).then_inc(row_max_done, 1)

            def body(c, par, new, one, two, nxt):
                for i in range(STEPS):
                    steps = steps_of(c, i, one, two)
                    if i == 0 and one:
                        routed_product(c - 1, EXPERTS - 1, 1 - par)
                    if i == 2 and one:
                        residual(c - 1, 1 - par, 0)
                    if i > 8 and new:
                        routed_product(c, i - 9, par)
                    for back, r in steps[:1]:
                        split_h(c - back, r, par if back == 2 else 1 - par)
                    if i == 0 and one:
                        low(c - 1, BLOCKS - 1)
                    if i == 2 and one:
                        residual(c - 1, 1 - par, 1)
                        low_x1(c - 1, 1 - par, 0)
                        low_x1(c - 1, 1 - par, 1)
                    if i in (2, 4, 6, 8) and new:
                        shared_product(c, i // 2 - 1)
                    if i in (1, 3, 5, 7) and new:
                        half_silu(c, i // 2)
                    if i in (3, 4, 6, 8) and new:
                        low(c, {3: 0, 4: 1, 6: 2, 8: 3}[i])
                    if i > 8 and new:
                        low(c, SHARED + i - 9)
                    for back, r in steps[1:]:
                        split_h(c - back, r, par if back == 2 else 1 - par)
                    if i == 3 and two:
                        output(c - 2, par)
                    if i == 4 and known(c, 0):
                        low_x(1, 1)
                    if known(c, 0):
                        for piece in {1: (1,), 2: (2, 3), 3: (4,), 4: (5, 6)}.get(i, ()):
                            routing(0, 0, piece)
                        if i == 8:
                            factors_of_wh()
                    if i == 6 and nxt:
                        logits(c + 1)
                    if i >= 8 and i < 15 and nxt:
                        routing(c + 1, 1 - par, i - 8)

            schedule(dve, prologue, body)


def kernel(x, cond_1024, L0_cond_router_w, L0_cond_router_t_w, L0_cond_router_bias, L0_cond_sw1,
           L0_cond_sw3, L0_cond_sw2, L0_cond_rw1, L0_cond_rw2, L1_cond_Wx, L1_cond_Wh, L1_cond_b):
    import numpy as np
    import concourse.bacc as bacc
    from concourse.bass_utils import run_bass_kernel_spmd

    def rows(a):
        a = np.asarray(a).reshape(KT, P, -1)
        return a.transpose(1, 0, 2).reshape(P, -1)

    def cols(a):
        return rows(np.asarray(a).T)

    x_np = np.asarray(x).reshape(BATCH, CHUNKS, STEPS, KT, P).transpose(1, 4, 3, 2, 0)
    x_np = np.ascontiguousarray(x_np).reshape(CHUNKS * P, KT * TOK)
    sw2, rw1, rw2 = np.asarray(L0_cond_sw2), np.asarray(L0_cond_rw1), np.asarray(L0_cond_rw2)
    w_np = np.concatenate([
        cols(L0_cond_sw1), cols(L0_cond_sw3),
        sw2.T.reshape(SHARED, P, DIM).transpose(1, 0, 2).reshape(P, -1),
        rw1.reshape(EXPERTS, P, KT, P).transpose(3, 0, 2, 1).reshape(P, -1),
        rw2.transpose(2, 0, 1).reshape(P, -1),
        rows(L1_cond_Wx)], axis=1)
    bias = np.broadcast_to(np.asarray(L0_cond_router_bias)[None, :], (P, EXPERTS))
    rank = np.broadcast_to(np.arange(EXPERTS, 0, -1, dtype=np.float32)[None, :], (P, EXPERTS))
    s_np = np.concatenate([rows(L1_cond_Wh), cols(cond_1024), cols(L0_cond_router_w), cols(L0_cond_router_t_w),
                           bias, rank], axis=1)

    nc = bacc.Bacc("TRN2", target_bir_lowering=False, num_devices=1)
    arrays = {"x_in": x_np, "w_in": np.ascontiguousarray(w_np), "s_in": np.ascontiguousarray(s_np),
              "b_in": np.asarray(L1_cond_b).reshape(1, DIM)}
    ins = [nc.dram_tensor(n, a.shape, F32, kind="ExternalInput").ap() for n, a in arrays.items()]
    scratch = nc.dram_tensor("scratch", (2 * EXPERTS, TOK), F32, kind="Internal").ap()
    out = nc.dram_tensor("out", (CHUNKS * P, KT * TOK), F32, kind="ExternalOutput").ap()
    moe_rnn(nc, *ins, scratch, out)
    got = run_bass_kernel_spmd(nc, [arrays], core_ids=[0]).results[0]["out"]
    got = got.reshape(CHUNKS, P, KT, STEPS, BATCH).transpose(4, 0, 3, 2, 1)
    return np.ascontiguousarray(got).reshape(BATCH, TIME, DIM)
```

```python
from contextlib import ExitStack

import concourse.bass as bass
from concourse import mybir

F32 = mybir.dt.float32
F32R = mybir.dt.float32r
BF16 = mybir.dt.bfloat16
F16 = mybir.dt.float16
ALU = mybir.AluOpType
ACT = mybir.ActivationFunctionType
AX = mybir.AxisListType

P = 128
BATCH, TIME, DIM = 32, 256, 256
EXPERTS = 8
HIDDEN_SHARED = 512
STEPS = 16
TOK = STEPS * BATCH
CHUNKS = TIME // STEPS
KT = DIM // P
SHARED = HIDDEN_SHARED // P
BLOCKS = SHARED + EXPERTS
TILES = 2 * SHARED + EXPERTS
LAG = 4
EPS = 1e-9
H_SCALE = 2.0 ** 15
W_SCALE = 2.0 ** 14
PRODUCTS = [[0, 1], [0]]
EXPONENT = 0x7F800000
BIAS_ROWS = 96
RING = [0, 1, 2] * 5 + [1]
W1, W3, W2, R1, R2, WX = 0, 1024, 2048, 3072, 5120, 7168
W_COLS = 7680
GROUP = 1024
GROUPS = [(a, min(a + GROUP, W_COLS)) for a in range(0, W_COLS, GROUP)]
WH, COND, RW, RT, RB, RANK = 0, 512, 576, 592, 608, 616
S_COLS = 624
DOWN = {0: [(10, (0, 1), 1)], 1: [(11, (0, 1), 1)],
        4: [(0, (0,), 0)], 5: [(0, (1,), 0)], 6: [(1, (0,), 0)], 7: [(1, (1,), 0)],
        8: [(2, (0, 1), 0)], 9: [(3, (0, 1), 0)],
        **{10 + e: [(4 + e, (0, 1), 0)] for e in range(6)}}
LATE = {**{i: DOWN[i] for i in (0, 1, 4, 5, 6, 7, 8, 9)},
        **{11 + e: [(4 + e, (0, 1), 0)] for e in range(5)}}
AFTER_LATE = {0: [(9, (0, 1), 1), (10, (0, 1), 1)]}
FIRST_HALF, SECOND_HALF = CHUNKS - 1, CHUNKS
LAST_COLUMNS = slice(TOK - BATCH, TOK)
STORES = [CHUNKS // 2 + 2, CHUNKS // 2]
ROUTER_OPS = 27
LOGIT_OPS = 3
FIRST_GATES = 2
SCALE_OPS, WH_OPS, B_OPS = 5, 5, 11


def moe_rnn(nc, x_in, w_in, s_in, b_in, scratch, out):
    with ExitStack() as ctx:
        def sb(name, shape, dt=F32):
            return ctx.enter_context(nc.sbuf_tensor(name, shape, dt))

        def pb(name, shape):
            return ctx.enter_context(nc.psum_tensor(name, shape, F32))

        def sem(name):
            return ctx.enter_context(nc.semaphore(name))

        w_raw = sb("w_raw", [P, W_COLS - 4 * GROUP])
        w_hi = sb("w_hi", [P, W_COLS], F32R)
        w_lo = sb("w_lo", [P, W_COLS], F32R)
        small = sb("small", [P, S_COLS])
        x = [sb(f"x{p}", [P, KT, TOK]) for p in range(2)]
        x_hi = [sb(f"x_hi{p}", [P, KT, TOK], F32R) for p in range(2)]
        x_lo = [sb(f"x_lo{p}", [P, KT, TOK], F32R) for p in range(2)]
        x1 = [sb(f"x1_{p}", [P, KT, TOK]) for p in range(2)]
        x1_hi = sb("x1_hi", [P, KT, TOK], F32R)
        x1_lo = sb("x1_lo", [P, KT, TOK], F32R)
        h = [sb(f"h{p}", [P, KT, TOK]) for p in range(2)]
        h_part = [[sb(f"h_part{n}_{s}", [P, KT, BATCH], F16) for s in range(2)] for n in range(2)]
        wh_part = [sb(f"wh_part{n}", [P, KT * DIM], F16) for n in range(2)]
        zero = sb("zero", [P, 1])
        row_max = sb("row_max", [P, 1])
        wh_max = sb("wh_max", [P, 1])
        wh_inv = sb("wh_inv", [P, 1])
        x_factor = sb("x_factor", [P, 1])
        tanh_scale = sb("tanh_scale", [P, 1])
        wh_rest = sb("wh_rest", [P, KT * DIM])
        b_raw = sb("b_raw", [BIAS_ROWS, DIM])
        b_part = [sb(f"b_part{n}", [BIAS_ROWS, DIM], BF16) for n in range(3)]
        b_rows = sb("b_rows", [BIAS_ROWS, DIM], BF16)
        ones = sb("ones", [BIAS_ROWS, TOK], BF16)
        gate_bc = [sb(f"gate_bc{p}", [P, EXPERTS, TOK]) for p in range(2)]
        g = [sb(f"g{i}", [P, TOK]) for i in range(2)]
        u = sb("u", [P, TOK])
        hs = [sb(f"hs{i}", [P, TOK]) for i in range(2)]
        hs_hi = [sb(f"hs_hi{i}", [P, TOK], F32R) for i in range(3)]
        hs_lo = [sb(f"hs_lo{i}", [P, TOK], F32R) for i in range(3)]
        rw_pad = sb("rw_pad", [P, KT, P], F32R)
        t_bias = sb("t_bias", [BATCH, EXPERTS])
        route_t = sb("route_t", [BATCH, STEPS, 32])
        logit = sb("logit", [BATCH, STEPS, EXPERTS])
        score = sb("score", [BATCH, STEPS, EXPERTS])
        sel = sb("sel", [BATCH, STEPS, EXPERTS])
        hit = sb("hit", [BATCH, STEPS, EXPERTS])
        first = sb("first", [BATCH, STEPS, EXPERTS])
        second = sb("second", [BATCH, STEPS, EXPERTS])
        top = sb("top", [BATCH, STEPS])
        den = sb("den", [BATCH, STEPS])
        inv = sb("inv", [BATCH, STEPS])
        big = sb("big", [BATCH, STEPS])
        comb = sb("comb", [BATCH, STEPS, 32])
        comb_t = [sb(f"comb_t{p}", [32, TOK]) for p in range(2)]
        gelu_probe = sb("gelu_probe", [BATCH, 1])

        up = [pb(f"up{i}", [P, TOK]) for i in range(3)]
        acc = [pb(f"acc{m}", [P, TOK]) for m in range(KT)]
        rec = pb("rec", [P, KT, TOK])
        route = pb("route", [P, 512])

        small_loaded = sem("small_loaded")
        w_loaded = [sem(f"w_loaded{i}") for i in range(len(GROUPS))]
        x_loaded = [sem(f"x_loaded{p}") for p in range(2)]
        comb_stored = sem("comb_stored")
        gate_loaded = [sem(f"gate_loaded{p}") for p in range(2)]
        first_gates_loaded = sem("first_gates_loaded")
        out_stored = [sem(f"out_stored{p}") for p in range(2)]
        w_hi_done = sem("w_hi_done")
        w_lo_done = sem("w_lo_done")
        w_rest_done = sem("w_rest_done")
        rw_cleared = sem("rw_cleared")
        rw_hi_done = sem("rw_hi_done")
        rw_lo_done = sem("rw_lo_done")
        zero_set = sem("zero_set")
        comb_cleared = sem("comb_cleared")
        x_hi_done = sem("x_hi_done")
        x_lo_done = sem("x_lo_done")
        t_bias_done = sem("t_bias_done")
        t_bias_copied = sem("t_bias_copied")
        route_done = sem("route_done")
        score_done = sem("score_done")
        router_step = sem("router_step")
        up_done = sem("up_done")
        down_done = sem("down_done")
        act_done = sem("act_done")
        u_done = sem("u_done")
        hs_done = sem("hs_done")
        hi_done = sem("hi_done")
        lo_done = sem("lo_done")
        x1_done = sem("x1_done")
        x1_hi_done = sem("x1_hi_done")
        x1_lo_done = sem("x1_lo_done")
        wx_done = sem("wx_done")
        rec_done = sem("rec_done")
        h_done = sem("h_done")
        part_done = [sem(f"part{n}_done") for n in range(2)]
        b_loaded = sem("b_loaded")
        row_max_done = sem("row_max_done")
        wh_max_done = sem("wh_max_done")
        scale_step = sem("scale_step")
        wx_scaled = sem("wx_scaled")
        wh_step = sem("wh_step")
        b_step = sem("b_step")
        out_done = sem("out_done")

        block = ctx.enter_context(nc.Block())

        def schedule(eng, prologue, body):
            prologue()
            body(0, 0, new=True, one=False, two=False, nxt=True)
            body(1, 1, new=True, one=True, two=False, nxt=True)
            body(2, 0, new=True, one=True, two=True, nxt=True)
            with eng.Fori(1, CHUNKS // 2 - 1) as pair:
                body(pair * 2 + 1, 1, new=True, one=True, two=True, nxt=True)
                body(pair * 2 + 2, 0, new=True, one=True, two=True, nxt=True)
            body(FIRST_HALF, 1, new=True, one=True, two=True, nxt=False)
            body(SECOND_HALF, 0, new=True, one=True, two=True, nxt=False)
            body(SECOND_HALF + 1, 1, new=False, one=True, two=True, nxt=False)
            body(SECOND_HALF + 2, 0, new=False, one=False, two=True, nxt=False)

        def steps_of(c, i, one, two):
            if known(c, SECOND_HALF) and i >= LAG:
                return [(1, i - LAG)] if i < LAG + STEPS // 2 else []
            if known(c, SECOND_HALF + 1):
                return [(2, i - LAG + STEPS // 2)] if LAG <= i < LAG + STEPS // 2 else []
            if i < LAG:
                return [(2, STEPS - LAG + i)] if two and not known(c, SECOND_HALF + 2) else []
            return [(1, i - LAG)] if one else []

        def columns(c):
            if known(c, FIRST_HALF):
                return slice(0, TOK // 2)
            return slice(TOK // 2, TOK) if known(c, SECOND_HALF) else slice(0, TOK)

        def early_columns(c):
            cols = columns(c)
            return slice(cols.start, LAST_COLUMNS.start) if known(c, SECOND_HALF) else cols

        def width(c):
            return columns(c).stop - columns(c).start

        def buf(c, par):
            return 1 if known(c, SECOND_HALF) else par

        def raw(n):
            a, b = GROUPS[n]
            if R1 <= a < WX:
                return gate_bc[1][:, :, :].rearrange("p e n -> p (e n)")[:, a - R1:b - R1]
            return w_raw[:, a:b] if a < R1 else w_raw[:, a - 4 * GROUP:b - 4 * GROUP]

        def known(c, n):
            return isinstance(c, int) and c == n

        def below(c, n):
            return isinstance(c, int) and c < n

        def nth(c, par):
            return c * 8 + (16 - 8 * par)

        @block.sync
        def _(sp):
            def load_x(c, par):
                sp.dma_start(x[par][:, :, :], x_in[bass.ts(c, P), :].rearrange("p (k n) -> p k n", k=KT)
                             ).then_inc(x_loaded[par], 16)

            def load_w(n):
                a, b = GROUPS[n]
                sp.dma_start(raw(n), w_in[:, a:b]).then_inc(w_loaded[n], 16)

            def store(c, par, cols):
                rows = bass.ts(CHUNKS - 1 if known(c, SECOND_HALF) else c, P)
                sp.dma_start(out[rows, :].rearrange("p (k n) -> p k n", k=KT)[:, :, cols],
                             x1[buf(c, par)][:, :, cols]).then_inc(out_stored[par], 16)

            def gates(c, par):
                sp.wait_ge(router_step, c * ROUTER_OPS + ROUTER_OPS)
                if not below(c, 2):
                    sp.wait_ge(gate_loaded[par], nth(c - 2, par))
                rows = scratch[par * EXPERTS:(par + 1) * EXPERTS, :]
                sp.dma_start(rows, comb_t[par][0:EXPERTS, :]).then_inc(comb_stored, 16)
                sp.wait_ge(comb_stored, c * 16 + 16)
                if not below(c, 2):
                    sp.wait_ge(hs_done, c * BLOCKS - BLOCKS)
                if known(c, 1):
                    sp.wait_ge(w_rest_done, 6)
                flat = rows.rearrange("(o e) n -> o (e n)", o=1)
                into = gate_bc[par][:, :, :].rearrange("p e n -> p (e n)")
                early = FIRST_GATES * TOK if known(c, 0) else 0
                if early:
                    sp.dma_start(into[:, 0:early], flat[:, 0:early].broadcast_to([P, early])
                                 ).then_inc(first_gates_loaded, 16)
                sp.dma_start(into[:, early:], flat[:, early:].broadcast_to([P, EXPERTS * TOK - early])
                             ).then_inc(gate_loaded[par], 16)

            def prologue():
                load_x(0, 0)
                load_w(0)
                load_w(1)
                load_x(1, 1)
                for n in range(2, len(GROUPS)):
                    load_w(n)

            def body(c, par, new, one, two, nxt):
                if known(c, 0):
                    gates(0, 0)
                if nxt and not known(c, 0):
                    sp.wait_ge(x1_done, c * KT)
                    load_x(c + 1, 1 - par)
                if two:
                    sp.wait_ge(out_done, c - 1)
                    store(c - 2, par, early_columns(c - 2))
                if known(c - 2, SECOND_HALF):
                    sp.wait_ge(out_done, c)
                    store(c - 2, par, LAST_COLUMNS)
                if nxt:
                    gates(c + 1, 1 - par)

            schedule(sp, prologue, body)
            for par in range(2):
                sp.wait_ge(out_stored[par], 16 * STORES[par])

        @block.tensor
        def _(pe):
            def with_high(dst, col, hi, start):
                for n, w in enumerate((w_hi, w_lo)):
                    pe.matmul(dst, w[:, col:col + P], hi, start=start and n == 0, stop=False,
                              skip_group_check=True)

            def with_low(dst, col, lo, stop, inc=None):
                mm = pe.matmul(dst, w_hi[:, col:col + P], lo, start=False, stop=stop,
                               skip_group_check=True)
                if inc is not None:
                    mm.then_inc(inc, 1)

            def router(c, par):
                if known(c, 0):
                    pe.wait_ge(rw_lo_done, 1)
                    pe.wait_ge(t_bias_copied, 1)
                else:
                    pe.wait_ge(router_step, c * ROUTER_OPS + (1 - ROUTER_OPS))
                for part, done in ((x_hi, x_hi_done), (x_lo, x_lo_done)):
                    pe.wait_ge(done, c + 1)
                    for k in range(KT):
                        mm = pe.matmul(route[:, :], rw_pad[:, k, :], part[par][:, k, :],
                                       start=(k == 0 and part is x_hi),
                                       stop=(k == KT - 1 and part is x_lo))
                mm.then_inc(route_done, 1)

            def recur(q, r):
                cols = slice(r * BATCH, (r + 1) * BATCH)
                if known(q, 0) and r == 0:
                    pe.wait_ge(wh_step, 1)
                    for m in range(KT):
                        for k in range(KT):
                            mm = pe.matmul(rec[:, m, cols],
                                           small[:, WH + k * DIM + m * P:WH + k * DIM + (m + 1) * P],
                                           small[:, COND + k * BATCH:COND + (k + 1) * BATCH],
                                           start=False, stop=(k == KT - 1), skip_group_check=True)
                    mm.then_inc(rec_done, 1)
                    return
                if known(q, 0) and r == 1:
                    pe.wait_ge(wh_step, WH_OPS)
                for n in range(2):
                    pe.wait_ge(part_done[n], q * STEPS + r)
                    for m in range(KT):
                        for k in range(KT):
                            for w in PRODUCTS[n]:
                                mm = pe.matmul(rec[:, m, cols],
                                               wh_part[w][:, k * DIM + m * P:k * DIM + (m + 1) * P],
                                               h_part[n][(r - 1) % 2][:, k, :], start=False,
                                               stop=(n == 1 and k == KT - 1 and w == PRODUCTS[1][-1]),
                                               skip_group_check=True)
                mm.then_inc(rec_done, 1)

            def input_part(q):
                if known(q, 0):
                    pe.wait_ge(b_step, B_OPS)
                else:
                    pe.wait_ge(h_done, FIRST_HALF * STEPS + STEPS // 2 if known(q, SECOND_HALF)
                               else q * STEPS)
                cols = columns(q)
                for m in range(KT):
                    pe.matmul(rec[:, m, cols], b_rows[:, m * P:(m + 1) * P], ones[:, cols],
                              start=True, stop=False, skip_group_check=True)
                for k in range(KT):
                    pe.wait_ge(x1_hi_done, q * KT + (k + 1))
                    for m in range(KT):
                        with_high(rec[:, m, cols], WX + k * DIM + m * P, x1_hi[:, k, cols], False)
                    pe.wait_ge(x1_lo_done, q * KT + (k + 1))
                    for m in range(KT):
                        last = k == KT - 1 and m == KT - 1
                        with_low(rec[:, m, cols], WX + k * DIM + m * P, x1_lo[:, k, cols], False,
                                 wx_done if last else None)

            def up_waits(c, i):
                back, prev = 0, i - 1
                while RING[prev % TILES] != RING[i]:
                    prev -= 1
                if prev < 0:
                    back, prev = 1, prev + TILES
                if not (known(c, 0) and back):
                    if prev >= 2 * SHARED:
                        pe.wait_ge(act_done, c * BLOCKS + (prev - SHARED + 1 - back * BLOCKS))
                    elif prev % 2:
                        pe.wait_ge(hs_done, c * BLOCKS + (prev // 2 + 1 - back * BLOCKS))
                    else:
                        pe.wait_ge(u_done, c * SHARED + (prev // 2 + 1 - back * SHARED))
                if i == 0 and not known(c, SECOND_HALF):
                    pe.wait_ge(x_lo_done, c + 1)
                if known(c, 0):
                    if i == 0:
                        pe.wait_ge(w_lo_done, 1)
                    if i == 1:
                        pe.wait_ge(w_rest_done, 1)
                    if i in (8, 12):
                        pe.wait_ge(w_rest_done, i // 4 + 1)

            def up_tile(c, i, par, ks):
                if ks[0] == 0:
                    up_waits(c, i)
                for k in ks:
                    if i < 2 * SHARED:
                        col = (W3 if i % 2 else W1) + k * HIDDEN_SHARED + (i // 2) * P
                    else:
                        col = R1 + (i - 2 * SHARED) * DIM + k * P
                    with_high(up[RING[i]][:, 0:width(c)], col, x_hi[buf(c, par)][:, k, columns(c)],
                              k == 0)
                    with_low(up[RING[i]][:, 0:width(c)], col, x_lo[buf(c, par)][:, k, columns(c)],
                             k == KT - 1, up_done if k == KT - 1 else None)

            def down_table(c):
                if known(c, 0) or known(c, FIRST_HALF):
                    return LATE
                if known(c, 1):
                    return {**DOWN, **AFTER_LATE}
                if known(c, SECOND_HALF) or known(c, SECOND_HALF + 1):
                    return {**LATE, **AFTER_LATE}
                return DOWN

            def down(c, b, ms):
                n = width(c)
                start = (W2 + b * DIM) if b < SHARED else (R2 + (b - SHARED) * DIM)
                if ms[0] == 0:
                    pe.wait_ge(hi_done, c * BLOCKS + (b + 1))
                    if b == 0 and not known(c, 0):
                        pe.wait_ge(x1_done, c * KT)
                    if known(c, 0) and b in (0, 4, 8):
                        pe.wait_ge(w_rest_done, {0: 2, 4: 5, 8: 6}[b])
                for m in ms:
                    with_high(acc[m][:, 0:n], start + m * P, hs_hi[b % 3][:, 0:n], b == 0)
                pe.wait_ge(lo_done, c * BLOCKS + (b + 1))
                for m in ms:
                    with_low(acc[m][:, 0:n], start + m * P, hs_lo[b % 3][:, 0:n], b == BLOCKS - 1,
                             down_done if m == KT - 1 else None)

            def prologue():
                pe.wait_ge(small_loaded, 16)
                for k in range(KT):
                    mm = pe.matmul(route[0:BATCH, 0:EXPERTS],
                                   small[:, COND + k * BATCH:COND + (k + 1) * BATCH],
                                   small[:, RT + k * EXPERTS:RT + (k + 1) * EXPERTS],
                                   start=(k == 0), stop=(k == KT - 1))
                mm.then_inc(t_bias_done, 1)
                router(0, 0)

            def body(c, par, new, one, two, nxt):
                for i in range(STEPS):
                    for back, r in steps_of(c, i, one, two):
                        recur(c - back, r)
                    if i == 1 and one:
                        down(c - 1, BLOCKS - 1, (0, 1))
                    if new and i == 3:
                        up_tile(c, 3, par, (1,))
                    elif new:
                        up_tile(c, i, par, (0, 1))
                    if new and i == 2:
                        up_tile(c, 3, par, (0,))
                    if i == (7 if known(c, 0) else 6) and nxt:
                        router(c + 1, 1 - par)
                    for b, ms, back in down_table(c).get(i, []):
                        if back and one and i != 1:
                            down(c - 1, b, ms)
                        if not back and new:
                            down(c, b, ms)
                    if i == LAG - 1 and one:
                        if known(c, 1):
                            pe.wait_ge(w_rest_done, 7)
                        input_part(c - 1)

            schedule(pe, prologue, body)

        @block.scalar
        def _(act):
            def split_w(n):
                a, b = GROUPS[n]
                act.wait_ge(w_loaded[n], 16)
                if n == len(GROUPS) - 1:
                    act.wait_ge(wx_scaled, 1)
                act.copy(w_hi[:, a:b], raw(n)).then_inc(w_hi_done, 1)

            def split_x(c, par):
                act.wait_ge(x_loaded[par], nth(c, par))
                act.copy(x_hi[par][:, :, :], x[par][:, :, :]).then_inc(x_hi_done, 1)

            def squash(c, b):
                tile = 2 * b if b < SHARED else b + SHARED
                act.wait_ge(up_done, c * TILES + (tile + 1))
                if not (known(c, 0) and b < 2):
                    act.wait_ge(hs_done, c * BLOCKS + (b - 1))
                n = width(c)
                if b < SHARED:
                    ins = act.activation(g[b % 2][:, 0:n], up[RING[tile]][:, 0:n], ACT.Tanh, scale=0.5)
                else:
                    ins = act.activation(g[b % 2][:, 0:n], up[RING[tile]][:, 0:n], ACT.Gelu)
                ins.then_inc(act_done, 1)

            def high(c, b):
                act.wait_ge(hs_done, c * BLOCKS + (b + 1))
                if not (known(c, 0) and b < 3):
                    act.wait_ge(down_done, c * BLOCKS + (b - 2))
                act.copy(hs_hi[b % 3][:, 0:width(c)], hs[b % 2][:, 0:width(c)]).then_inc(hi_done, 1)

            def recur(q, r, par):
                if r == 0 and not below(q, 2):
                    act.wait_ge(out_done, q - 1)
                act.wait_ge(rec_done, q * STEPS + (r + 1))
                if known(q, 0) and r == 0:
                    act.wait_ge(scale_step, SCALE_OPS)
                cols = slice(r * BATCH, (r + 1) * BATCH)
                act.activation(h[par][:, :, cols], rec[:, :, cols], ACT.Tanh, scale=tanh_scale[:, :]
                               ).then_inc(h_done, 1)

            def sigmoid(c):
                act.wait_ge(router_step, c * ROUTER_OPS + LOGIT_OPS)
                act.activation(score[:, :, :], logit[:, :, :], ACT.Sigmoid).then_inc(score_done, 1)

            def load_gelu(c):
                act.wait_ge(score_done, c + 1)
                act.activation(gelu_probe[:, :], score[:, 0, 0:1], ACT.Gelu)

            def prologue():
                act.dma_start(small[:, :], s_in[:, :]).then_inc(small_loaded, 16)
                act.dma_start(b_raw[:, :], b_in.broadcast_to([BIAS_ROWS, DIM])).then_inc(b_loaded, 16)
                act.wait_ge(zero_set, 1)
                act.activation(gelu_probe[:, :], zero[0:BATCH, :], ACT.Gelu)
                act.wait_ge(rw_cleared, 1)
                act.wait_ge(small_loaded, 16)
                act.copy(rw_pad[:, :, 0:EXPERTS],
                         small[:, RW:RW + KT * EXPERTS].rearrange("p (k e) -> p k e", k=KT)
                         ).then_inc(rw_hi_done, 1)
                split_x(0, 0)
                split_w(0)
                split_w(1)
                sigmoid(0)

            def body(c, par, new, one, two, nxt):
                for i in range(STEPS):
                    if i == 0 and one:
                        squash(c - 1, BLOCKS - 1)
                    if new and i in (1, 3, 5, 7):
                        squash(c, i // 2)
                    if new and i > 8:
                        squash(c, SHARED + i - 9)
                    for back, r in steps_of(c, i, one, two):
                        recur(c - back, r, par if back == 2 else 1 - par)
                    if i == 0 and one:
                        high(c - 1, BLOCKS - 1)
                    if i in (2, 3) and one:
                        cols = columns(c - 1)
                        for k in (i - 2,):
                            act.wait_ge(x1_done, c * KT - KT + (k + 1))
                            if not known(c, 1):
                                act.wait_ge(wx_done, c - 1)
                            act.copy(x1_hi[:, k, cols], x1[buf(c - 1, 1 - par)][:, k, cols]
                                     ).then_inc(x1_hi_done, 1)
                    if new and i in (3, 4, 6, 8):
                        high(c, {3: 0, 4: 1, 6: 2, 8: 3}[i])
                    if new and i > 8:
                        high(c, SHARED + i - 9)
                    if known(c, 0):
                        if i in (0, 2, 3, 5, 6, 14):
                            split_w({0: 2, 2: 3, 3: 4, 5: 5, 6: 6, 14: 7}[i])
                    if i == (8 if known(c, 0) else 7) and nxt:
                        sigmoid(c + 1)
                    if i == 8 and nxt:
                        load_gelu(c + 1)

            schedule(act, prologue, body)

        @block.gpsimd
        def _(pool):
            pool.memset(rw_pad[:, :, :].bitcast(F32), 0.0).then_inc(rw_cleared, 1)
            pool.memset(comb[:, :, :], 0.0).then_inc(comb_cleared, 1)
            pool.memset(zero[:, :], 0.0).then_inc(zero_set, 1)
            pool.memset(b_rows[:, :], 0.0).then_inc(b_step, 1)
            pool.memset(ones[:, :], 1.0).then_inc(b_step, 1)

            def low_w(n):
                a, b = GROUPS[n]
                pool.wait_ge(w_hi_done, n + 1)
                pool.tensor_tensor(w_lo[:, a:b], raw(n), w_hi[:, a:b].bitcast(F32), ALU.subtract
                                   ).then_inc(w_rest_done, 1)

            zeros = zero[:, :].rearrange("p (k n) -> p k n", k=1).broadcast_to([P, KT, TOK])

            def split_x(c, par):
                pool.wait_ge(x_loaded[par], nth(c, par))
                if not below(c, 2):
                    pool.wait_ge(up_done, c * TILES - TILES)
                pool.tensor_tensor(x_hi[par][:, :, :], x[par][:, :, :], zeros, ALU.add
                                   ).then_inc(x_hi_done, 1)
                pool.wait_ge(x_hi_done, c + 1)
                pool.tensor_tensor(x_lo[par][:, :, :], x[par][:, :, :], x_hi[par][:, :, :].bitcast(F32),
                                   ALU.subtract).then_inc(x_lo_done, 1)

            def prologue():
                pool.wait_ge(zero_set, 1)
                for n in (1, 2, 3, 4):
                    low_w(n)
                split_x(1, 1)
                for n in (5, 6):
                    low_w(n)
                pool.wait_ge(row_max_done, 1)
                nc.gpsimd.partition_all_reduce(wh_max[:, :], row_max[:, :], P, bass.bass_isa.ReduceOp.max
                                               ).then_inc(wh_max_done, 1)
                pool.wait_ge(scale_step, SCALE_OPS)
                pool.wait_ge(w_loaded[-1], 16)
                pool.tensor_scalar(raw(len(GROUPS) - 1), raw(len(GROUPS) - 1), x_factor[:, :], None, ALU.mult
                                   ).then_inc(wx_scaled, 1)
                wh = small[:, WH:WH + KT * DIM]
                pool.tensor_scalar(wh, wh, x_factor[:, :], None, ALU.mult).then_inc(wh_step, 1)
                pool.wait_ge(b_loaded, 16)
                pool.tensor_scalar(b_raw[:, :], b_raw[:, :], x_factor[0:BIAS_ROWS, :], None, ALU.mult
                                   ).then_inc(b_step, 1)
                pool.wait_ge(wh_step, 1)
                pool.tensor_scalar(wh_rest[:, :], wh, 1.0 / H_SCALE, None, ALU.mult).then_inc(wh_step, 1)
                pool.wait_ge(wh_step, 2)
                pool.tensor_copy(wh_part[0][:, :], wh_rest[:, :]).then_inc(wh_step, 1)
                pool.wait_ge(wh_step, 3)
                pool.tensor_tensor(wh_rest[:, :], wh_rest[:, :], wh_part[0][:, :], ALU.subtract
                                   ).then_inc(wh_step, 1)
                pool.wait_ge(wh_step, 4)
                pool.tensor_copy(wh_part[1][:, :], wh_rest[:, :]).then_inc(wh_step, 1)
                for n in range(3):
                    pool.wait_ge(b_step, 3 + 2 * n)
                    pool.tensor_copy(b_part[n][:, :], b_raw[:, :]).then_inc(b_step, 1)
                    if n < 2:
                        pool.wait_ge(b_step, 4 + 2 * n)
                        pool.tensor_tensor(b_raw[:, :], b_raw[:, :], b_part[n][:, :], ALU.subtract
                                           ).then_inc(b_step, 1)
                pool.wait_ge(b_step, 8)
                for n in range(3):
                    if n:
                        pool.wait_ge(b_step, 8 + n)
                    pool.tensor_copy(b_rows[32 * n:32 * n + 1, :], b_part[n][32 * n:32 * n + 1, :]
                                     ).then_inc(b_step, 1)
                pool.wait_ge(b_step, B_OPS)
                low_w(len(GROUPS) - 1)

            def body(c, par, new, one, two, nxt):
                if nxt and not known(c, 0):
                    split_x(c + 1, 1 - par)

            schedule(pool, prologue, body)

        @block.vector
        def _(dve):
            def low_w(n):
                a, b = GROUPS[n]
                dve.wait_ge(w_hi_done, n + 1)
                dve.tensor_tensor(w_lo[:, a:b], raw(n), w_hi[:, a:b].bitcast(F32), ALU.subtract
                                  ).then_inc(w_lo_done, 1)

            def low_x(c, par):
                dve.wait_ge(x_hi_done, c + 1)
                dve.tensor_tensor(x_lo[par][:, :, :], x[par][:, :, :], x_hi[par][:, :, :].bitcast(F32),
                                  ALU.subtract).then_inc(x_lo_done, 1)

            def half_silu(c, j):
                dve.wait_ge(act_done, c * BLOCKS + (j + 1))
                if j:
                    dve.wait_ge(hs_done, c * BLOCKS + j)
                n = width(c)
                dve.scalar_tensor_tensor(out=u[:, 0:n], in0=g[j % 2][:, 0:n], scalar=1.0,
                                         in1=up[RING[2 * j]][:, 0:n], op0=ALU.add, op1=ALU.mult
                                         ).then_inc(u_done, 1)

            def shared_product(c, j):
                dve.wait_ge(u_done, c * SHARED + (j + 1))
                dve.wait_ge(up_done, c * TILES + (2 * j + 2))
                n = width(c)
                dve.scalar_tensor_tensor(out=hs[j % 2][:, 0:n], in0=u[:, 0:n], scalar=0.5,
                                         in1=up[RING[2 * j + 1]][:, 0:n], op0=ALU.mult, op1=ALU.mult
                                         ).then_inc(hs_done, 1)

            def routed_product(c, e, par):
                b = SHARED + e
                if known(c, 0) and e == 0:
                    dve.wait_ge(first_gates_loaded, 16)
                if e == (FIRST_GATES if known(c, 0) else 0) and not known(c, SECOND_HALF):
                    dve.wait_ge(gate_loaded[par], nth(c, par))
                dve.wait_ge(act_done, c * BLOCKS + (b + 1))
                n = width(c)
                dve.tensor_tensor(hs[b % 2][:, 0:n], g[b % 2][:, 0:n],
                                  gate_bc[buf(c, par)][:, e, columns(c)], ALU.mult
                                  ).then_inc(hs_done, 1)

            def low(c, b):
                dve.wait_ge(hi_done, c * BLOCKS + (b + 1))
                n = width(c)
                dve.tensor_tensor(hs_lo[b % 3][:, 0:n], hs[b % 2][:, 0:n], hs_hi[b % 3][:, 0:n].bitcast(F32),
                                  ALU.subtract).then_inc(lo_done, 1)

            def each(a):
                return a.rearrange("p (t o) -> p t o", o=1).broadcast_to([BATCH, STEPS, EXPERTS])

            def per_expert(a):
                return a.rearrange("p (o e) -> p o e", o=1).broadcast_to([BATCH, STEPS, EXPERTS])

            def logits(c):
                base = c * ROUTER_OPS
                dve.wait_ge(route_done, c + 1)
                if known(c, 0):
                    dve.wait_ge(t_bias_copied, 1)
                dve.transpose(route_t[:, :, :].rearrange("p s r -> p (s r)"), route[0:32, :]
                              ).then_inc(router_step, 1)
                dve.wait_ge(router_step, base + 1)
                dve.tensor_tensor(logit[:, :, :], route_t[:, :, 0:EXPERTS],
                                  route_t[:, :, EXPERTS:2 * EXPERTS], ALU.add).then_inc(router_step, 1)
                dve.wait_ge(router_step, base + 2)
                dve.tensor_tensor(logit[:, :, :], logit[:, :, :], per_expert(t_bias[:, :]), ALU.add
                                  ).then_inc(router_step, 1)

            def selection(c):
                dve.wait_ge(score_done, c + 1)
                dve.tensor_tensor(sel[:, :, :], score[:, :, :],
                                  per_expert(small[0:BATCH, RB:RB + EXPERTS]), ALU.add
                                  ).then_inc(router_step, 1)

            def reach(c, n):
                base = c * ROUTER_OPS + n
                dve.wait_ge(router_step, base)
                dve.tensor_reduce(top[:, :], sel[:, :, :], AX.X, ALU.max).then_inc(router_step, 1)
                dve.wait_ge(router_step, base + 1)
                dve.tensor_tensor(hit[:, :, :], sel[:, :, :], each(top[:, :]), ALU.is_equal
                                  ).then_inc(router_step, 1)
                dve.wait_ge(router_step, base + 2)
                dve.tensor_tensor(hit[:, :, :], hit[:, :, :],
                                  per_expert(small[0:BATCH, RANK:RANK + EXPERTS]), ALU.mult
                                  ).then_inc(router_step, 1)

            def lowest(c, n, one):
                base = c * ROUTER_OPS + n
                dve.wait_ge(router_step, base)
                dve.tensor_reduce(top[:, :], hit[:, :, :], AX.X, ALU.max).then_inc(router_step, 1)
                dve.wait_ge(router_step, base + 1)
                dve.tensor_tensor(one[:, :, :], hit[:, :, :], each(top[:, :]), ALU.is_equal
                                  ).then_inc(router_step, 1)

            def strike_first(c):
                dve.wait_ge(router_step, c * ROUTER_OPS + 9)
                dve.scalar_tensor_tensor(out=sel[:, :, :], in0=first[:, :, :], scalar=-3.0e38,
                                         in1=sel[:, :, :], op0=ALU.mult, op1=ALU.add
                                         ).then_inc(router_step, 1)

            def picked_sum(c):
                base = c * ROUTER_OPS
                dve.wait_ge(router_step, base + 15)
                dve.tensor_tensor(second[:, :, :], first[:, :, :], second[:, :, :], ALU.add
                                  ).then_inc(router_step, 1)
                dve.wait_ge(router_step, base + 16)
                if known(c, 0):
                    dve.wait_ge(comb_cleared, 1)
                dve.tensor_tensor(comb[:, :, 0:EXPERTS], second[:, :, :], score[:, :, :], ALU.mult
                                  ).then_inc(router_step, 1)
                dve.wait_ge(router_step, base + 17)
                dve.tensor_reduce(den[:, :], comb[:, :, 0:EXPERTS], AX.X, ALU.add
                                  ).then_inc(router_step, 1)
                dve.wait_ge(router_step, base + 18)
                dve.tensor_scalar(inv[:, :], den[:, :], EPS, None, ALU.add).then_inc(router_step, 1)
                dve.tensor_scalar(big[:, :], den[:, :], EPS, None, ALU.is_gt).then_inc(router_step, 1)

            def factors(c):
                base = c * ROUTER_OPS
                dve.wait_ge(router_step, base + 19)
                dve.reciprocal(inv[:, :], inv[:, :]).then_inc(router_step, 1)
                dve.wait_ge(router_step, base + 21)
                dve.tensor_tensor(inv[:, :], inv[:, :], big[:, :], ALU.mult).then_inc(router_step, 1)
                dve.tensor_scalar(big[:, :], big[:, :], -0.5, 0.5, ALU.mult, ALU.add
                                  ).then_inc(router_step, 1)

            def combine(c, par):
                base = c * ROUTER_OPS
                dve.wait_ge(router_step, base + 23)
                dve.tensor_tensor(comb[:, :, 0:EXPERTS], comb[:, :, 0:EXPERTS], each(inv[:, :]), ALU.mult
                                  ).then_inc(router_step, 1)
                dve.tensor_tensor(second[:, :, :], second[:, :, :], each(big[:, :]), ALU.mult
                                  ).then_inc(router_step, 1)
                dve.wait_ge(router_step, base + 25)
                dve.tensor_tensor(comb[:, :, 0:EXPERTS], comb[:, :, 0:EXPERTS], second[:, :, :], ALU.add
                                  ).then_inc(router_step, 1)
                dve.wait_ge(router_step, base + 26)
                if not below(c, 2):
                    dve.wait_ge(comb_stored, c * 16 - 16)
                dve.transpose(comb_t[par][:, :], comb[:, :, :].rearrange("p t e -> p (t e)")
                              ).then_inc(router_step, 1)

            def routing(c, par, piece):
                if piece == 0:
                    selection(c)
                    reach(c, 4)
                if piece == 1:
                    lowest(c, 7, first)
                    strike_first(c)
                if piece == 2:
                    reach(c, 10)
                if piece == 3:
                    lowest(c, 13, second)
                if piece == 4:
                    picked_sum(c)
                if piece == 5:
                    factors(c)
                if piece == 6:
                    combine(c, par)

            def residual(c, par, m):
                if m == 0:
                    dve.wait_ge(down_done, c * BLOCKS + BLOCKS)
                    if not below(c, 2) and not known(c, SECOND_HALF):
                        dve.wait_ge(out_stored[par], nth(c - 2, par))
                at, cols = buf(c, par), columns(c)
                dve.scalar_tensor_tensor(out=x1[at][:, m, cols], in0=acc[m][:, 0:width(c)],
                                         scalar=1.0 / 3.0, in1=x[at][:, m, cols], op0=ALU.mult, op1=ALU.add
                                         ).then_inc(x1_done, 1)

            def low_x1(c, par, k):
                dve.wait_ge(x1_hi_done, c * KT + (k + 1))
                cols = columns(c)
                dve.tensor_tensor(x1_lo[:, k, cols], x1[buf(c, par)][:, k, cols],
                                  x1_hi[:, k, cols].bitcast(F32), ALU.subtract).then_inc(x1_lo_done, 1)

            def add_h(c, par, cols):
                at = buf(c, par)
                dve.tensor_tensor(x1[at][:, :, cols], x1[at][:, :, cols], h[at][:, :, cols], ALU.add
                                  ).then_inc(out_done, 1)

            def output(c, par):
                if known(c, SECOND_HALF):
                    dve.wait_ge(h_done, CHUNKS * STEPS)
                    add_h(c, par, LAST_COLUMNS)
                else:
                    dve.wait_ge(h_done, c * STEPS + (STEPS // 2 if known(c, FIRST_HALF) else STEPS))
                    add_h(c, par, columns(c))

            def split_h(q, r, par):
                if not (known(q, CHUNKS - 1) and r == STEPS - 1):
                    cols = slice(r * BATCH, (r + 1) * BATCH)
                    parts = [h_part[n][r % 2][:, :, :] for n in range(2)]
                    dve.wait_ge(h_done, q * STEPS + (r + 1))
                    dve.tensor_scalar(parts[0], h[par][:, :, cols], H_SCALE, None, ALU.mult
                                      ).then_inc(part_done[0], 1)
                    dve.wait_ge(part_done[0], q * STEPS + (r + 1))
                    dve.scalar_tensor_tensor(out=parts[1], in0=h[par][:, :, cols], scalar=H_SCALE,
                                             in1=parts[0], op0=ALU.mult, op1=ALU.subtract
                                             ).then_inc(part_done[1], 1)

            def factors_of_wh():
                i32 = mybir.dt.int32
                dve.wait_ge(wh_max_done, 1)
                dve.tensor_scalar(wh_max[:, :], wh_max[:, :], 2.0 ** -60, 2.0 ** 90, ALU.max, ALU.min
                                  ).then_inc(scale_step, 1)
                dve.wait_ge(scale_step, 1)
                dve.tensor_scalar(wh_max[:, :].bitcast(i32), wh_max[:, :].bitcast(i32), EXPONENT, None,
                                  ALU.bitwise_and).then_inc(scale_step, 1)
                dve.wait_ge(scale_step, 2)
                dve.tensor_scalar(wh_inv[:, :].bitcast(i32), wh_max[:, :].bitcast(i32), -1.0,
                                  float(254 << 23), ALU.mult, ALU.add).then_inc(scale_step, 1)
                dve.tensor_scalar(tanh_scale[:, :], wh_max[:, :], 1.0 / (H_SCALE * W_SCALE), None,
                                  ALU.mult).then_inc(scale_step, 1)
                dve.wait_ge(scale_step, 3)
                dve.tensor_scalar(x_factor[:, :], wh_inv[:, :], H_SCALE * W_SCALE, None, ALU.mult
                                  ).then_inc(scale_step, 1)

            def prologue():
                dve.wait_ge(t_bias_done, 1)
                dve.tensor_copy(t_bias[:, :], route[0:BATCH, 0:EXPERTS]).then_inc(t_bias_copied, 1)
                dve.wait_ge(rw_hi_done, 1)
                dve.tensor_tensor(rw_pad[:, :, EXPERTS:2 * EXPERTS],
                                  small[:, RW:RW + KT * EXPERTS].rearrange("p (k e) -> p k e", k=KT),
                                  rw_pad[:, :, 0:EXPERTS].bitcast(F32), ALU.subtract
                                  ).then_inc(rw_lo_done, 1)
                low_x(0, 0)
                low_w(0)
                logits(0)
                routing(0, 0, 0)

            def body(c, par, new, one, two, nxt):
                for i in range(STEPS):
                    if i == 0 and one:
                        routed_product(c - 1, EXPERTS - 1, 1 - par)
                    if i == 2 and one:
                        residual(c - 1, 1 - par, 0)
                    if i > 8 and new:
                        routed_product(c, i - 9, par)
                    for back, r in steps_of(c, i, one, two):
                        split_h(c - back, r, par if back == 2 else 1 - par)
                    if i == 0 and one:
                        low(c - 1, BLOCKS - 1)
                    if i == 2 and one:
                        residual(c - 1, 1 - par, 1)
                        low_x1(c - 1, 1 - par, 0)
                    if i == 3 and one:
                        low_x1(c - 1, 1 - par, 1)
                    if i in (2, 4, 6, 8) and new:
                        shared_product(c, i // 2 - 1)
                    if i in (1, 3, 5, 7) and new:
                        half_silu(c, i // 2)
                    if i in (3, 4, 6, 8) and new:
                        low(c, {3: 0, 4: 1, 6: 2, 8: 3}[i])
                    if i > 8 and known(c, 0):
                        routing(1, 1, i - 9)
                    if i > 8 and new:
                        low(c, SHARED + i - 9)
                    if i == LAG + STEPS // 2 - 2 and known(c, SECOND_HALF + 1):
                        add_h(c - 1, 1 - par, early_columns(c - 1))
                    if i == 3 and two:
                        output(c - 2, par)
                    if known(c, 0):
                        for piece in {1: (1,), 2: (2, 3), 3: (4,), 4: (5,), 5: (6,)}.get(i, ()):
                            routing(0, 0, piece)
                        if i == 6:
                            dve.tensor_reduce(row_max[:, :], small[:, WH:WH + KT * DIM], AX.X, ALU.max,
                                              apply_absolute_value=True).then_inc(row_max_done, 1)
                        if i == 8:
                            factors_of_wh()
                    if i == (7 if known(c, 0) else 6) and nxt:
                        logits(c + 1)
                    if 8 <= i < 15 and nxt and not known(c, 0):
                        routing(c + 1, 1 - par, i - 8)

            schedule(dve, prologue, body)


def kernel(x, cond_1024, L0_cond_router_w, L0_cond_router_t_w, L0_cond_router_bias, L0_cond_sw1,
           L0_cond_sw3, L0_cond_sw2, L0_cond_rw1, L0_cond_rw2, L1_cond_Wx, L1_cond_Wh, L1_cond_b):
    import numpy as np
    import concourse.bacc as bacc
    from concourse.bass_utils import run_bass_kernel_spmd

    def rows(a):
        a = np.asarray(a).reshape(KT, P, -1)
        return a.transpose(1, 0, 2).reshape(P, -1)

    def cols(a):
        return rows(np.asarray(a).T)

    x_np = np.asarray(x).reshape(BATCH, CHUNKS, STEPS, KT, P).transpose(1, 4, 3, 2, 0)
    x_np = np.ascontiguousarray(x_np).reshape(CHUNKS * P, KT * TOK)
    sw2, rw1, rw2 = np.asarray(L0_cond_sw2), np.asarray(L0_cond_rw1), np.asarray(L0_cond_rw2)
    w_np = np.concatenate([
        cols(L0_cond_sw1), cols(L0_cond_sw3),
        sw2.T.reshape(SHARED, P, DIM).transpose(1, 0, 2).reshape(P, -1),
        rw1.reshape(EXPERTS, P, KT, P).transpose(3, 0, 2, 1).reshape(P, -1),
        rw2.transpose(2, 0, 1).reshape(P, -1),
        rows(L1_cond_Wx)], axis=1)
    bias = np.broadcast_to(np.asarray(L0_cond_router_bias)[None, :], (P, EXPERTS))
    rank = np.broadcast_to(np.arange(EXPERTS, 0, -1, dtype=np.float32)[None, :], (P, EXPERTS))
    s_np = np.concatenate([rows(L1_cond_Wh), cols(cond_1024), cols(L0_cond_router_w), cols(L0_cond_router_t_w),
                           bias, rank], axis=1)

    nc = bacc.Bacc("TRN2", target_bir_lowering=False, num_devices=1)
    arrays = {"x_in": x_np, "w_in": np.ascontiguousarray(w_np), "s_in": np.ascontiguousarray(s_np),
              "b_in": np.asarray(L1_cond_b).reshape(1, DIM)}
    ins = [nc.dram_tensor(n, a.shape, F32, kind="ExternalInput").ap() for n, a in arrays.items()]
    scratch = nc.dram_tensor("scratch", (2 * EXPERTS, TOK), F32, kind="Internal").ap()
    out = nc.dram_tensor("out", (CHUNKS * P, KT * TOK), F32, kind="ExternalOutput").ap()
    moe_rnn(nc, *ins, scratch, out)
    got = run_bass_kernel_spmd(nc, [arrays], core_ids=[0]).results[0]["out"]
    got = got.reshape(CHUNKS, P, KT, STEPS, BATCH).transpose(4, 0, 3, 2, 1)
    return np.ascontiguousarray(got).reshape(BATCH, TIME, DIM)
```
